# Optimizing a Trainium2 kernel written in Bass

```python
import numpy as np
import jax
import jax.numpy as jnp

def _softmax(x, axis=-1):
    return jax.nn.softmax(x, axis=axis)

def _gelu(x):
    return jax.nn.gelu(x, approximate=True)

def _silu(x):
    return jax.nn.silu(x)

def _sigmoid(x):
    return jax.nn.sigmoid(x)

def _layernorm(x, axis=-1, eps=1e-05):
    m = jnp.mean(x, axis=axis, keepdims=True)
    v = jnp.var(x, axis=axis, keepdims=True)
    return (x - m) / jnp.sqrt(v + eps)

def _scatter_add(tgt, idx, src, axis=0):
    return tgt.at[idx].add(src)

def _segment_sum(src, seg, n):
    return jax.ops.segment_sum(src, seg, n)
kernel_name = 'mk_flamingo_gated_d1_seqx_r2_7afba2'

def setup_inputs(seed: int=0):
    np.random.seed(seed)
    _w = jnp.asarray

    def _rec_inputs():
        import jax
        import jax.numpy as jnp
        _rk = jax.random.key(seed)
        x = -0.0002928 + 1 * jax.random.normal(jax.random.fold_in(_rk, 1), (8, 512, 1024), jnp.float32)
        _lenS = 512 - jax.random.randint(jax.random.fold_in(_rk, 7), (8,), 0, max(1, 512 // 4) + 1, jnp.int32)
        _lenS2 = 512 - jax.random.randint(jax.random.fold_in(_rk, 8), (8,), 0, max(1, 512 // 4) + 1, jnp.int32)
        _ctx_2048P = jax.random.normal(jax.random.fold_in(_rk, 11), (8, 16, 1024), jnp.float32)
        _ctx_2048c = jax.random.dirichlet(jax.random.fold_in(_rk, 511), 0.3 * jnp.ones((16,), jnp.float32), (8, 512))
        _ctx_2048t = jnp.einsum('bsk,bkd->bsd', _ctx_2048c, _ctx_2048P)
        _ctx_2048t = _ctx_2048t * jax.lax.rsqrt(jnp.mean(jnp.square(_ctx_2048t)) + 1e-12) * 0.953939
        ctx_2048 = -1.39393e-06 + 0.999914 * (_ctx_2048t + 0.3 * jax.random.normal(jax.random.fold_in(_rk, 611), (8, 512, 1024), jnp.float32))
        _validS = jnp.arange(512)[None, :] < _lenS[:, None]
        _validS2 = jnp.arange(512)[None, :] < _lenS2[:, None]
        _causal = jnp.tril(jnp.ones((512, 512), dtype=bool))
        mask_Bx1x2048_fk1 = jnp.where(jnp.ones((8, 1, 1024), dtype=bool), 1.0, 0.0).astype(jnp.float32)
        _g = jax.random.normal(jax.random.fold_in(_rk, 9001), (2, 1), jnp.float32)
        _g = jnp.sign(_g) * jnp.maximum(jnp.abs(_g), 1.0) + (_g == 0) * 1.0
        g_xattn = _g[0]
        g_ffn = _g[1]
        return (x, ctx_2048, mask_Bx1x2048_fk1, g_xattn, g_ffn)
    x, ctx_2048, mask_Bx1x2048_fk1, g_xattn, g_ffn = _rec_inputs()

    def _L0_xattn_setup():
        import math
        import jax, jax.numpy as jnp
        import numpy as np
        SIZE = 512
        HEADS = 16
        HEAD_DIM = SIZE // HEADS
        B, T, S = (2, 1024, 1024)
        NEG = 1000000.0
        key = jax.random.key(seed)
        ks = jax.random.split(key, 10)
        target = jax.random.normal(ks[0], (B, SIZE, T), dtype=jnp.float32)
        source = jax.random.normal(ks[1], (B, SIZE, S), dtype=jnp.float32)
        target_mask = (jax.random.uniform(ks[2], (B, 1, T)) > 0.1).astype(jnp.float32)
        source_mask = (jax.random.uniform(ks[3], (B, 1, S)) > 0.1).astype(jnp.float32)
        scale = 1.0 / math.sqrt(SIZE)
        Wq = jax.random.normal(ks[4], (SIZE, SIZE), dtype=jnp.float32) * scale
        Wk = jax.random.normal(ks[5], (SIZE, SIZE), dtype=jnp.float32) * scale
        Wv = jax.random.normal(ks[6], (SIZE, SIZE), dtype=jnp.float32) * scale
        bq = jax.random.normal(ks[7], (SIZE,), dtype=jnp.float32) * 0.01
        bk = jax.random.normal(ks[8], (SIZE,), dtype=jnp.float32) * 0.01
        bv = jax.random.normal(ks[9], (SIZE,), dtype=jnp.float32) * 0.01
        return {'target': target, 'source': source, 'target_mask': target_mask, 'source_mask': source_mask, 'Wq': Wq, 'bq': bq, 'Wk': Wk, 'bk': bk, 'Wv': Wv, 'bv': bv}
    _L0_xattn_all = _L0_xattn_setup()
    _L0_xattn_in = {k: v for k, v in _L0_xattn_all.items() if k in ('Wq', 'bq', 'Wk', 'bk', 'Wv', 'bv')}
    del _L0_xattn_all

    def _L0_ffn_setup():
        import jax, jax.numpy as jnp
        import numpy as np
        FP8 = jnp.float8_e4m3fn
        key = jax.random.key(seed)
        k1, k2 = jax.random.split(key)
        input1 = jax.random.normal(k1, (2, 2048, 1024), dtype=jnp.float32)
        input2 = jax.random.normal(k2, (1024, 1024), dtype=jnp.float32)
        scale = jnp.array(0.5, dtype=jnp.float32)
        scale1 = jnp.array(0.5, dtype=jnp.float32)
        return {'input1': input1, 'input2': input2, 'scale': scale, 'scale1': scale1}
    _L0_ffn_all = _L0_ffn_setup()
    _L0_ffn_in = {k: v for k, v in _L0_ffn_all.items() if k in ('input2', 'scale', 'scale1')}
    del _L0_ffn_all
    return {'x': x, 'ctx_2048': ctx_2048, 'mask_Bx1x2048_fk1': mask_Bx1x2048_fk1, 'g_xattn': g_xattn, 'g_ffn': g_ffn, 'L0_xattn_Wq': _L0_xattn_in['Wq'], 'L0_xattn_bq': _L0_xattn_in['bq'], 'L0_xattn_Wk': _L0_xattn_in['Wk'], 'L0_xattn_bk': _L0_xattn_in['bk'], 'L0_xattn_Wv': _L0_xattn_in['Wv'], 'L0_xattn_bv': _L0_xattn_in['bv'], 'L0_ffn_input2': _L0_ffn_in['input2'], 'L0_ffn_scale': _L0_ffn_in['scale'], 'L0_ffn_scale1': _L0_ffn_in['scale1']}

def reference(x, ctx_2048, mask_Bx1x2048_fk1, g_xattn, g_ffn, L0_xattn_Wq, L0_xattn_bq, L0_xattn_Wk, L0_xattn_bk, L0_xattn_Wv, L0_xattn_bv, L0_ffn_input2, L0_ffn_scale, L0_ffn_scale1):
    import jax
    import jax.numpy as jnp

    def _L0_xattn_ref(target, source, target_mask, source_mask, Wq, bq, Wk, bk, Wv, bv):
        import math
        import jax, jax.numpy as jnp
        import numpy as np
        SIZE = 512
        HEADS = 16
        HEAD_DIM = SIZE // HEADS
        B, T, S = (2, 1024, 1024)
        NEG = 1000000.0
        b, _, t = target.shape
        s = source.shape[-1]
        q = jnp.einsum('oc,bct->bot', Wq, target) + bq[None, :, None]
        k = jnp.einsum('oc,bcs->bos', Wk, source) + bk[None, :, None]
        v = jnp.einsum('oc,bcs->bos', Wv, source) + bv[None, :, None]
        q = q.reshape(b, HEADS, HEAD_DIM, t)
        k = k.reshape(b, HEADS, HEAD_DIM, s)
        v = v.reshape(b, HEADS, HEAD_DIM, s)
        dot = jnp.einsum('bhdt,bhds->bhts', q, k) / math.sqrt(HEAD_DIM)
        mask = target_mask[:, :, :, None] * source_mask[:, :, None, :]
        dot = mask * dot - (1.0 - mask) * NEG
        amap = jax.nn.softmax(dot, axis=-1) * mask
        out = jnp.einsum('bhts,bhds->bhdt', amap, v)
        return out.reshape(b, HEADS * HEAD_DIM, t)

    def _L0_ffn_ref(input1, input2, scale, scale1):
        import jax, jax.numpy as jnp
        import numpy as np
        FP8 = jnp.float8_e4m3fn
        q1 = (input1 * scale).astype(FP8)
        q2 = (input2 * scale1).astype(FP8)
        d1 = q1.astype(jnp.float32) * (1.0 / scale)
        d2 = q2.astype(jnp.float32) * (1.0 / scale1)
        return jnp.einsum('bmk,kn->bmn', d1, d2)
    x = x + jnp.tanh(g_xattn[0]) * _L0_xattn_ref(_layernorm(x, axis=-1), ctx_2048, mask_Bx1x2048_fk1, mask_Bx1x2048_fk1, L0_xattn_Wq, L0_xattn_bq, L0_xattn_Wk, L0_xattn_bk, L0_xattn_Wv, L0_xattn_bv)
    x = x + jnp.tanh(g_ffn[0]) * _L0_ffn_ref(_layernorm(x, axis=-1), L0_ffn_input2, L0_ffn_scale, L0_ffn_scale1)
    return x

_drawn_inputs = setup_inputs


def setup_inputs(seed=0):
    import zlib

    import numpy as np

    out = dict(_drawn_inputs(seed))
    spreads = {}
    factors = {'L0_xattn_bq': 42.156, 'L0_xattn_bk': 200.0, 'L0_xattn_bv': 200.0}
    for name, (base, spread) in spreads.items():
        noise = np.random.default_rng([zlib.crc32(name.encode()), seed]).standard_normal(out[name].shape)
        drawn = base * np.exp(spread * noise) if base else spread * noise
        out[name] = jnp.asarray(drawn.astype(out[name].dtype))
    for name, factor in factors.items():
        out[name] = (out[name] * factor).astype(out[name].dtype)
    return out
```

```python
from contextlib import ExitStack

import concourse.bass as bass
from concourse import mybir

ALU = mybir.AluOpType
ACT = mybir.ActivationFunctionType
AX = mybir.AxisListType.X
F32 = mybir.dt.float32
F32R = mybir.dt.float32r
BF16 = mybir.dt.bfloat16
U32 = mybir.dt.uint32

P = 128
HALF = 512
EPS = 1e-5

NEG_Q, NEG_K = 8000.0, 125.0

EXPONENT_BITS = 0x7F800000
F8_MIN_NORMAL = 2.0 ** -6
ROUND_TO_4_BITS = 1.5 * 2.0 ** 20
F8_OVERFLOW = 2.0 ** 120 / 1.8


def counted(value):
    return not isinstance(value, int) or value > 0


def flamingo_gated_layer(nc, x, ctx, mask, g_xattn, g_ffn, Wq, bq, Wk, bk, Wv, bv, W2, scale, scale1, out):
    B, C, T = x.shape
    S = ctx.shape[2]
    HEADS, D = 16, C // 16
    CB = C // P
    QH = P // D
    QUADS = C // P
    NQ = B * QUADS
    SJ = S // P
    TH = T // HALF
    TC = HALF // P
    KC = T // P
    INV_SQRT_D = 1.0 / float(D) ** 0.5
    assert (C, T, S, D, TH) == (512, 1024, 1024, 32, 2)

    x_rows = x.rearrange("b c t -> (b c) t")
    out_rows = out.rearrange("b c t -> (b c) t")

    q_scr = nc.dram_tensor("q_scr", [2, B * C, T], F32, kind="Internal").ap()
    k_scr = nc.dram_tensor("k_scr", [2, B * C, S], F32, kind="Internal").ap()
    v_scr = nc.dram_tensor("v_scr", [NQ, S, P], F32, kind="Internal").ap()
    inv_scr = nc.dram_tensor("inv_scr", [TH, QH, HALF], F32, kind="Internal").ap()
    qx_scr = nc.dram_tensor("qx_scr", [2, B, QUADS, T], F32, kind="Internal").ap()
    kx_scr = nc.dram_tensor("kx_scr", [2, B, QUADS, S], F32, kind="Internal").ap()
    tm_scr = nc.dram_tensor("tm_scr", [B, QUADS, T], F32, kind="Internal").ap()

    ctxs = ExitStack()
    with ctxs:
        def sem(name, stack=ctxs):
            return stack.enter_context(nc.semaphore(name))

        def sb(name, shape, dt, stack=ctxs):
            return stack.enter_context(nc.sbuf_tensor(name, shape, dt))

        def pb(name, shape, dt, stack=ctxs):
            return stack.enter_context(nc.psum_tensor(name, shape, dt))

        ident_r = sb("ident_r", [P, P], F32R)
        ident_b = sb("ident_b", [P, P], BF16)
        ones = sb("ones", [P, D], F32)
        neg_half = sb("neg_half", [P, CB], F32)
        w2q = sb("w2q", [P, KC, T], BF16)
        g1 = sb("g1", [P, 1], F32)
        g2 = sb("g2", [P, 1], F32)
        scl = sb("scl", [P, 1], F32)
        scl1 = sb("scl1", [P, 1], F32)

        F8_STEPS = 6

        def f8_step(step, y, big, q, isnan):
            if step == 0:
                return nc.vector.tensor_scalar(big.bitcast(U32), y.bitcast(U32), EXPONENT_BITS, None, ALU.bitwise_and)
            if step == 1:
                return nc.vector.tensor_scalar(big, big, F8_MIN_NORMAL, ROUND_TO_4_BITS, ALU.max, ALU.mult)
            if step == 2:
                return nc.vector.tensor_tensor(y, y, big, ALU.add)
            if step == 3:
                return nc.vector.tensor_tensor(q, y, big, ALU.subtract)
            if step == 4:
                return nc.vector.tensor_scalar(isnan, q, F8_OVERFLOW, 0.0, ALU.mult, ALU.mult)
            return nc.vector.tensor_tensor(q, q, isnan, ALU.add)

        with ExitStack() as st:
            w_names = ("k", "v", "q")
            w_hi = {w: sb(f"w_hi_{w}", [P, CB, C], F32R, st) for w in w_names}
            w_lo = {w: sb(f"w_lo_{w}", [P, CB, C], F32R, st) for w in w_names}
            bias_q = sb("bias_q", [P, CB], F32, st)
            bias_k = sb("bias_k", [P, CB], F32, st)
            bias_v = sb("bias_v", [P, C], F32, st)
            sm_cols = sb("sm_cols", [P, B * SJ], F32, st)
            bank = [pb(f"bank{i}", [P, HALF], F32, st) for i in range(8)]

            with ExitStack() as su:
                w_nat = sb("w_nat", [P, 3, CB, C], F32, su)
                m_nat = sb("m_nat", [B * SJ, P], F32, su)
                m_rows = sb("m_rows", [B, T], F32, su)
                qx = sb("qx", [B, 2, T], F32R, su)
                kx = sb("kx", [B, 2, S], F32R, su)
                ident_f = sb("ident_f", [P, P], F32, su)
                gl = sb("gl", [P, 4], F32, su)
                gt = sb("gt", [P, 4], F32, su)
                w_loaded = [sem(f"w_loaded{i}", su) for i in range(3)]
                bias_loaded = sem("bias_loaded", su)
                mask_loaded = sem("mask_loaded", su)
                gates_loaded = sem("gates_loaded", su)
                ident_done = sem("ident_done", su)
                w_turned = sem("w_turned", su)
                hi_done = sem("hi_done", su)
                lo_done = sem("lo_done", su)
                m_turned = sem("m_turned", su)
                tanh_done = sem("tanh_done", su)
                chain_done = sem("setup_chain", su)
                extra_done = sem("extra_done", su)
                stored = sem("setup_stored", su)

                with nc.Block() as block:
                    @block.sync
                    def _(sp):
                        for n, w in enumerate((Wk, Wv, Wq)):
                            sp.dma_start(w_nat[:, n], w.rearrange("(a p) c -> p a c", p=P)).then_inc(w_loaded[n], 16)
                        sp.dma_start(m_nat[:, :], mask.rearrange("b o (j p) -> (b o j) p", p=P)).then_inc(mask_loaded, 16)
                        sp.dma_start(m_rows[:, :], mask.rearrange("b o t -> (b o) t")).then_inc(mask_loaded, 16)
                        sp.wait_ge(extra_done, 3)
                        for r in range(2):
                            for q in range(QUADS):
                                sp.dma_start(qx_scr[r, :, q, :], qx[:, r, :].bitcast(F32)).then_inc(stored, 16)
                                sp.dma_start(kx_scr[r, :, q, :], kx[:, r, :].bitcast(F32)).then_inc(stored, 16)
                        for q in range(QUADS):
                            sp.dma_start(tm_scr[:, q, :], m_rows[:, :]).then_inc(stored, 16)
                        sp.wait_ge(stored, 16 * 5 * QUADS)

                    @block.gpsimd
                    def _(pool):
                        pool.memset(ident_f[:, :], 0.0).then_inc(ident_done, 1)
                        pool.wait_ge(ident_done, 1)
                        pool.affine_select(out=ident_f[:, :], in_=ident_f[:, :], compare_op=ALU.not_equal, fill=1.0,
                                           base=0, pattern=[[-1, P]], channel_multiplier=1).then_inc(ident_done, 1)
                        pool.memset(ones[:, :], 1.0).then_inc(ident_done, 1)
                        pool.memset(neg_half[:, :], -0.5).then_inc(ident_done, 1)

                    @block.scalar
                    def _(act):
                        act.dma_start(bias_k[:, :], bk.rearrange("(a p) -> p a", p=P), allow_slow_non_contiguous=True).then_inc(bias_loaded, 16)
                        act.dma_start(bias_q[:, :], bq.rearrange("(a p) -> p a", p=P), allow_slow_non_contiguous=True).then_inc(bias_loaded, 16)
                        act.dma_start(bias_v[:, :], bv.partition_broadcast(P)).then_inc(bias_loaded, 16)
                        for n, g in enumerate((g_xattn, g_ffn, scale, scale1)):
                            act.dma_start(gl[:, n:n + 1], g.partition_broadcast(P)).then_inc(gates_loaded, 16)
                        act.wait_ge(gates_loaded, 64)
                        act.activation(gt[:, 0:2], gl[:, 0:2], ACT.Tanh).then_inc(tanh_done, 1)
                        for n, w in enumerate(w_names):
                            for cb in range(CB):
                                i = n * CB + cb
                                act.wait_ge(w_turned, i + 1)
                                act.activation(w_hi[w][:, cb], bank[i % 6][:, :], ACT.Copy).then_inc(hi_done, 1)
                        act.wait_ge(bias_loaded, 48)

                    @block.tensor
                    def _(pe):
                        pe.wait_ge(ident_done, 2)
                        for n in range(3):
                            pe.wait_ge(w_loaded[n], 16)
                            for cb in range(CB):
                                i = n * CB + cb
                                if counted(i - 5):
                                    pe.wait_ge(lo_done, i - 5)
                                for ob in range(CB):
                                    last = nc.tensor.transpose(bank[i % 6][:, ob * P:(ob + 1) * P],
                                                               w_nat[:, n, ob, cb * P:(cb + 1) * P], ident_f[:, :])
                                last.then_inc(w_turned, 1)
                        pe.wait_ge(mask_loaded, 32)
                        nc.tensor.transpose(bank[7][:, 0:B * SJ], m_nat[:, :], ident_f[0:B * SJ, 0:B * SJ]).then_inc(m_turned, 1)

                    @block.vector
                    def _(dve):
                        n_chain = [0]

                        def chain(ins):
                            n_chain[0] += 1
                            ins.then_inc(chain_done, 1)
                            dve.wait_ge(chain_done, n_chain[0])

                        dve.wait_ge(ident_done, 2)
                        chain(nc.vector.tensor_copy(ident_r[:, :], ident_f[:, :]))
                        chain(nc.vector.tensor_copy(ident_b[:, :], ident_f[:, :]))
                        for n, w in enumerate(w_names):
                            for cb in range(CB):
                                i = n * CB + cb
                                dve.wait_ge(hi_done, i + 1)
                                nc.vector.tensor_tensor(w_lo[w][:, cb], bank[i % 6][:, :], w_hi[w][:, cb].bitcast(F32),
                                                        ALU.subtract).then_inc(lo_done, 1)
                        dve.wait_ge(m_turned, 1)
                        chain(nc.vector.tensor_copy(sm_cols[:, :], bank[7][:, 0:B * SJ]))
                        chain(nc.vector.tensor_scalar(qx[:, 0, :], m_rows[:, :], -NEG_Q, None, ALU.mult))
                        nc.vector.tensor_scalar(qx[:, 1, :], m_rows[:, :], 1.0, NEG_Q, ALU.subtract, ALU.mult).then_inc(extra_done, 1)
                        nc.vector.tensor_scalar(kx[:, 0, :], m_rows[:, :], 1.0, -NEG_K, ALU.subtract, ALU.mult).then_inc(extra_done, 1)
                        nc.vector.tensor_scalar(kx[:, 1, :], m_rows[:, :], 0.0, NEG_K, ALU.mult, ALU.add).then_inc(extra_done, 1)
                        dve.wait_ge(tanh_done, 1)
                        chain(nc.vector.tensor_copy(g1[:, :], gt[:, 0:1]))
                        chain(nc.vector.tensor_copy(scl[:, :], gl[:, 2:3]))
                        chain(nc.vector.tensor_copy(scl1[:, :], gl[:, 3:4]))
                        chain(nc.vector.reciprocal(gt[:, 2:4], gl[:, 2:4]))
                        chain(nc.vector.tensor_tensor(gt[:, 2:3], gt[:, 2:3], gt[:, 3:4], ALU.mult))
                        chain(nc.vector.tensor_tensor(g2[:, :], gt[:, 1:2], gt[:, 2:3], ALU.mult))

            with ExitStack() as pr:
                c_raw = sb("c_raw", [P, CB, S], F32, pr)
                x_raw = sb("x_raw", [P, CB, T], F32, pr)
                c_hi = sb("c_hi", [P, CB, S], F32R, pr)
                c_lo = sb("c_lo", [P, CB, S], F32R, pr)
                xn = x_raw
                x_hi = sb("x_hi", [P, CB, T], F32R, pr)
                x_lo = sb("x_lo", [P, CB, T], F32R, pr)
                m_b = sb("m_b", [P, T], F32, pr)
                m_bs = sb("m_bs", [P, T], F32, pr)
                stats = sb("stats", [P, CB, 2, 6], F32, pr)
                mv = sb("mv", [P, CB, 2], F32, pr)
                sm_now = sb("sm_now", [P, SJ], F32, pr)
                credit = sb("credit", [P, 1], F32, pr)
                W2B = KC // B
                w2f = sb("w2f", [P, W2B, T], F32, pr)
                w2big = sb("w2big", [P, T], F32, pr)
                w2nan = sb("w2nan", [P, T], BF16, pr)
                w2_loaded = sem("w2_loaded", pr)
                w2_chain = sem("w2_chain", pr)
                w2_done = sem("w2_done", pr)
                ve = sb("ve", [P, CB], F32, pr)
                rstd = sb("rstd", [P, CB], F32, pr)
                STG = 4
                stage = sb("stage", [P, STG, HALF], F32, pr)
                stage_hi = sb("stage_hi", [P, 2, HALF], F32R, pr)
                stage_lo = sb("stage_lo", [P, 2, HALF], F32R, pr)
                c_loaded = [sem(f"c_loaded{i}", pr) for i in range(CB)]
                x_loaded = [sem(f"x_loaded{i}", pr) for i in range(CB)]
                m_loaded = sem("m_loaded", pr)
                chi_done = sem("chi_done", pr)
                clo_done = sem("clo_done", pr)
                xhi_done = sem("xhi_done", pr)
                xlo_done = sem("xlo_done", pr)
                xn_done = sem("xn_done", pr)
                stats_done = sem("stats_done", pr)
                ve_done = sem("ve_done", pr)
                rstd_done = sem("rstd_done", pr)
                sm_set = sem("sm_set", pr)
                mbs_done = sem("mbs_done", pr)
                group_done = sem("group_done", pr)
                evacuated = sem("evacuated", pr)
                v_masked = sem("v_masked", pr)
                v_stored = [sem(f"v_stored{i}", pr) for i in range(STG)]
                qk_hi = sem("qk_hi", pr)
                qk_lo = sem("qk_lo", pr)
                qk_stored = [sem(f"qk_stored{i}", pr) for i in range(2)]
                NB = len(bank)
                GK = CB * 2
                GV = SJ
                G = 2 * GK + GV

                def run(eng, batch):
                    batch(0, True)
                    if B > 2:
                        with eng.Fori(1, B - 1) as b:
                            batch(b, True)
                    batch(B - 1, False)

                with nc.Block() as block:
                    @block.gpsimd
                    def _(pool):
                        def batch(b, more):
                            pool.wait_ge(ve_done, b + 1)
                            nc.gpsimd.tensor_tensor(rstd[:, :], ve[:, :], neg_half[:, :], ALU.pow).then_inc(rstd_done, 1)
                            for e in range(2 * GK):
                                pool.wait_ge(qk_hi, b * 2 * GK + e + 1)
                                if counted(32 * (b * GK + e // 2)):
                                    pool.wait_ge(qk_stored[e % 2], 32 * (b * GK + e // 2))
                                g = e if e < GK else e + GV
                                nc.gpsimd.tensor_tensor(stage_lo[:, e % 2], stage[:, g % STG], stage_hi[:, e % 2].bitcast(F32),
                                                        ALU.subtract).then_inc(qk_lo, 1)

                        run(pool, batch)

                    @block.sync
                    def _(sp):
                        def batch(b, more):
                            if counted(b * G):
                                sp.wait_ge(evacuated, b * G)
                            sp.dma_start(m_b[:, :], mask[b, 0, :].partition_broadcast(P)).then_inc(m_loaded, 16)
                            for g in range(G):
                                if GK <= g < GK + GV:
                                    j = g - GK
                                    sp.wait_ge(v_masked, b * GV + j + 1)
                                    dst = v_scr[bass.ds(b * QUADS, QUADS), j * P:(j + 1) * P, :].rearrange("q s d -> s q d")
                                    src = stage[:, g % STG].rearrange("p (q d) -> p q d", q=QUADS)
                                    sp.dma_start(dst, src).then_inc(v_stored[g % STG], 16)
                                    continue
                                to, gg, e = (k_scr, g, g) if g < GK else (q_scr, g - GK - GV, g - GV)
                                s = slice((gg % 2) * HALF, (gg % 2 + 1) * HALF)
                                sp.wait_ge(qk_lo, b * 2 * GK + e + 1)
                                for part, src in ((0, stage_hi), (1, stage_lo)):
                                    sp.dma_start(to[part, bass.ds(b * C + (gg // 2) * P, P), s],
                                                 src[:, e % 2].bitcast(F32)).then_inc(qk_stored[e % 2], 16)

                        run(sp, batch)
                        for i in range(STG):
                            sp.wait_ge(v_stored[i], 16 * B * (GV // STG))
                        for i in range(2):
                            sp.wait_ge(qk_stored[i], 32 * B * GK)

                    @block.scalar
                    def _(act):
                        def load_ctx(b):
                            if counted(b * CB):
                                act.wait_ge(clo_done, b * CB)
                            for cb in range(CB):
                                act.dma_start(c_raw[:, cb], ctx[b, cb * P:(cb + 1) * P, :]).then_inc(c_loaded[cb], 16)

                        def load_x(b):
                            if counted(b * CB):
                                act.wait_ge(xlo_done, b * CB)
                            for cb in range(CB):
                                act.dma_start(x_raw[:, cb], x[b, cb * P:(cb + 1) * P, :]).then_inc(x_loaded[cb], 16)

                        def load_w2(b):
                            if counted(b):
                                act.wait_ge(w2_done, b)
                            act.dma_start(w2f[:, :, :], W2[bass.ds(b * (W2B * P), W2B * P), :].rearrange("(a p) n -> p a n", p=P)).then_inc(w2_loaded, 16)

                        def split_ctx(b):
                            if counted(b * G - GK):
                                act.wait_ge(group_done, b * G - GK)
                            for cb in range(CB):
                                act.wait_ge(c_loaded[cb], 16 * (b + 1))
                                nc.scalar.activation(c_hi[:, cb], c_raw[:, cb], ACT.Copy).then_inc(chi_done, 1)

                        def high(b, g):
                            e = g if g < GK else g - GV
                            act.wait_ge(evacuated, b * G + g + 1)
                            if counted(32 * (b * GK + e // 2)):
                                act.wait_ge(qk_stored[e % 2], 32 * (b * GK + e // 2))
                            nc.scalar.activation(stage_hi[:, e % 2], stage[:, g % STG], ACT.Copy).then_inc(qk_hi, 1)

                        def batch(b, more):
                            if more:
                                load_ctx(b + 1)
                            if counted(b * G):
                                act.wait_ge(group_done, b * G)
                            for cb in range(CB):
                                act.wait_ge(xn_done, b * CB + cb + 1)
                                nc.scalar.activation(x_hi[:, cb], xn[:, cb], ACT.Copy).then_inc(xhi_done, 1)
                            for g in range(GK):
                                high(b, g)
                            for g in range(GK, GK + GV):
                                j = g - GK
                                act.wait_ge(evacuated, b * G + g + 1)
                                nc.scalar.activation(stage[:, g % STG], stage[:, g % STG], ACT.Copy,
                                                     scale=sm_now[:, j:j + 1]).then_inc(v_masked, 1)
                            if more:
                                load_x(b + 1)
                                load_w2(b + 1)
                                split_ctx(b + 1)
                            for g in range(GK + GV, G):
                                high(b, g)

                        load_ctx(0)
                        load_x(0)
                        load_w2(0)
                        split_ctx(0)
                        run(act, batch)

                    @block.tensor
                    def _(pe):
                        def batch(b, more):
                            for g in range(G):
                                ready, hi, lo = (clo_done, c_hi, c_lo) if g < GK + GV else (xlo_done, x_hi, x_lo)
                                if counted(b * G + g + 1 - NB):
                                    pe.wait_ge(evacuated, b * G + g + 1 - NB)
                                acc = bank[g % NB][:, :]
                                for cb in range(CB):
                                    if g in (0, GK + GV):
                                        pe.wait_ge(ready, b * CB + cb + 1)
                                    if GK <= g < GK + GV:
                                        j = g - GK
                                        s = slice(j * P, (j + 1) * P)
                                        pairs = ((hi[:, cb, s], w_hi["v"][:, cb]), (lo[:, cb, s], w_hi["v"][:, cb]),
                                                 (hi[:, cb, s], w_lo["v"][:, cb]))
                                    else:
                                        w, gg = ("k", g) if g < GK else ("q", g - GK - GV)
                                        o = slice((gg // 2) * P, (gg // 2 + 1) * P)
                                        s = slice((gg % 2) * HALF, (gg % 2 + 1) * HALF)
                                        pairs = ((w_hi[w][:, cb, o], hi[:, cb, s]), (w_lo[w][:, cb, o], hi[:, cb, s]),
                                                 (w_hi[w][:, cb, o], lo[:, cb, s]))
                                    for n, (a, m) in enumerate(pairs):
                                        last = nc.tensor.matmul(acc, a, m, start=(cb == 0 and n == 0),
                                                                stop=(cb == CB - 1 and n == 2))
                                last.then_inc(group_done, 1)

                        run(pe, batch)

                    @block.vector
                    def _(dve):
                        def low_ctx(b):
                            for cb in range(CB):
                                dve.wait_ge(chi_done, b * CB + cb + 1)
                                nc.vector.tensor_tensor(c_lo[:, cb], c_raw[:, cb], c_hi[:, cb].bitcast(F32),
                                                        ALU.subtract).then_inc(clo_done, 1)

                        def evacuate(b, g):
                            dve.wait_ge(group_done, b * G + g + 1)
                            if GK <= g - STG < GK + GV:
                                dve.wait_ge(v_stored[g % STG], 16 * (b * (GV // STG) + (g - STG - GK) // STG + 1))
                            else:
                                if counted(b * 2 * GK + (g - STG if g < GK + STG else g - STG - GV) + 1):
                                    dve.wait_ge(qk_lo, b * 2 * GK + (g - STG if g < GK + STG else g - STG - GV) + 1)
                            acc, to = bank[g % NB][:, :], stage[:, g % STG]
                            if GK <= g < GK + GV:
                                nc.vector.tensor_tensor(to, acc, bias_v[:, :], ALU.add).then_inc(evacuated, 1)
                            else:
                                bias, m, gg = (bias_k, m_b, g) if g < GK else (bias_q, m_bs, g - GK - GV)
                                s = slice((gg % 2) * HALF, (gg % 2 + 1) * HALF)
                                nc.vector.scalar_tensor_tensor(to, acc, bias[:, gg // 2:gg // 2 + 1], m[:, s],
                                                               ALU.add, ALU.mult).then_inc(evacuated, 1)

                        def round_w2(b):
                            dve.wait_ge(w2_loaded, 16 * (b + 1))
                            for a in range(W2B):
                                wf = w2f[:, a]
                                q = w2q[:, bass.ds(b * W2B + a, 1), :].rearrange("p a n -> p (a n)")
                                done = (b * W2B + a) * (F8_STEPS + 1)
                                nc.vector.tensor_scalar(wf, wf, scl1[:, 0:1], None, ALU.mult).then_inc(w2_chain, 1)
                                for step in range(F8_STEPS):
                                    dve.wait_ge(w2_chain, done + step + 1)
                                    f8_step(step, wf, w2big[:, :], q, w2nan[:, :]).then_inc(w2_chain, 1)
                                dve.wait_ge(w2_chain, done + F8_STEPS + 1)
                            nc.vector.memset(credit[:, :], 0.0).then_inc(w2_done, 1)

                        def batch(b, more):
                            for cb in range(CB):
                                dve.wait_ge(x_loaded[cb], 16 * (b + 1))
                                for h in range(2):
                                    nc.vector.bn_stats(stats[:, cb, h], x_raw[:, cb, h * HALF:(h + 1) * HALF]).then_inc(stats_done, 1)
                            if counted(b * GV):
                                dve.wait_ge(v_masked, b * GV)
                            dve.wait_ge(stats_done, 3 * CB * b + 2 * CB)
                            nc.vector.tensor_copy(sm_now[:, :], sm_cols[:, bass.ds(b * SJ, SJ)]).then_inc(sm_set, 1)
                            for cb in range(CB):
                                nc.vector.bn_aggr(mv[:, cb], stats[:, cb]).then_inc(stats_done, 1)
                            dve.wait_ge(stats_done, 3 * CB * (b + 1))
                            nc.vector.tensor_scalar(ve[:, :], mv[:, :, 1], EPS, None, ALU.add).then_inc(ve_done, 1)
                            dve.wait_ge(rstd_done, b + 1)
                            for cb in range(CB):
                                nc.vector.tensor_scalar(xn[:, cb], x_raw[:, cb], mv[:, cb, 0:1], rstd[:, cb:cb + 1],
                                                        ALU.subtract, ALU.mult).then_inc(xn_done, 1)
                            dve.wait_ge(m_loaded, 16 * (b + 1))
                            if counted(b * G):
                                dve.wait_ge(evacuated, b * G)
                            nc.vector.tensor_scalar(m_bs[:, :], m_b[:, :], INV_SQRT_D, None, ALU.mult).then_inc(mbs_done, 1)
                            for g in range(GK // 2):
                                evacuate(b, g)
                            for cb in range(CB):
                                dve.wait_ge(xhi_done, b * CB + cb + 1)
                                nc.vector.tensor_tensor(x_lo[:, cb], xn[:, cb], x_hi[:, cb].bitcast(F32),
                                                        ALU.subtract).then_inc(xlo_done, 1)
                            for g in range(GK // 2, GK + GV // 2):
                                evacuate(b, g)
                            round_w2(b)
                            for g in range(GK + GV // 2, GK + GV):
                                evacuate(b, g)
                            if more:
                                low_ctx(b + 1)
                            dve.wait_ge(mbs_done, b + 1)
                            for g in range(GK + GV, G):
                                evacuate(b, g)

                        low_ctx(0)
                        run(dve, batch)

        with ExitStack() as at:
            NSLOT = 2 * SJ * QH
            KX, KS = 98, 100
            PR = 4
            XLEAD = 24

            k_st = [sb(f"k_st{i}", [P, QH, S], F32R, at) for i in range(2)]
            q_st = [sb(f"q_st{i}", [P, TH, QH, HALF], F32R, at) for i in range(2)]
            probs = sb("probs", [P, PR, QH, HALF], F32, at)
            pair_sum = sb("pair_sum", [P, 2, QH, HALF], F32, at)
            v_t = [sb(f"v_t{i}", [P, SJ, P], F32, at) for i in range(2)]
            part_max = sb("part_max", [P, TH, 2, QH * TC], F32, at)
            row_max = sb("row_max", [P, QH * TC], F32, at)
            neg_max = sb("neg_max", [P, P], F32R, at)
            max_rows = sb("max_rows", [2 * QH * TC, P], F32R, at)
            o_raw = sb("o_raw", [P, TH, HALF], F32, at)
            den = sb("den", [P, HALF], F32, at)
            den_c = sb("den_c", [P, HALF // 32], F32, at)
            inv_c = sb("inv_c", [P, HALF // 32], F32, at)
            tm_c = sb("tm_c", [P, TH, HALF // 32], F32, at)
            inv_b = sb("inv_b", [P, TH, HALF], F32, at)
            res = [sb(f"res{i}", [P, T], F32, at) for i in range(2)]
            y = sb("y", [P, T], F32, at)
            big = sb("big", [P, T], F32, at)
            y8 = sb("y8", [P, T], BF16, at)
            isnan = sb("isnan", [P, T], BF16, at)
            y8_t = sb("y8_t", [P, KC, P], BF16, at)
            st2 = sb("st2", [P, 2, 6], F32, at)
            mv2 = sb("mv2", [P, 2], F32, at)
            ve2 = sb("ve2", [P, 1], F32, at)
            rs2 = sb("rs2", [P, 1], F32, at)
            rss = sb("rss", [P, 1], F32, at)

            s_bank = [pb(f"s_bank{i}", [P, HALF], F32, at) for i in range(2)]
            x_bank = [pb(f"x_bank{i}", [P, HALF], F32, at) for i in range(2)]
            o_bank = pb("o_bank", [P, HALF], F32, at)
            d_bank = pb("d_bank", [P, HALF], F32, at)
            m_bank = pb("m_bank", [P, HALF], F32, at)
            f_bank = pb("f_bank", [P, HALF], F32, at)
            f_bank_b = f_bank[:, :].bitcast(BF16)

            init_done = sem("init_done", at)
            stacked = sem("stacked", at)
            v_loaded = [sem(f"v_loaded{i}", at) for i in range(2)]
            x_ready = sem("x_ready", at)
            max_done = sem("max_done", at)
            negmax_done = sem("negmax_done", at)
            max_turned = sem("max_turned", at)
            max_copied = sem("max_copied", at)
            max_set = sem("max_set", at)
            scores_ready = sem("scores_ready", at)
            exp_done = sem("exp_done", at)
            pair_done = sem("pair_done", at)
            pv_done = sem("pv_done", at)
            den_done = sem("den_done", at)
            o_copied = sem("o_copied", at)
            den_copied = sem("den_copied", at)
            den_moved = sem("den_moved", at)
            inv_done = sem("inv_done", at)
            inv_moved = sem("inv_moved", at)
            inv_spread = sem("inv_spread", at)
            tm_loaded = sem("tm_loaded", at)
            res_loaded = [sem(f"res_loaded{i}", at) for i in range(2)]
            norm_done = sem("norm_done", at)
            rs2_done = sem("rs2_done", at)
            y8_turned = sem("y8_turned", at)
            y8_copied = sem("y8_copied", at)
            ffn_done = sem("ffn_done", at)
            ffn_added = sem("ffn_added", at)
            out_stored = sem("out_stored", at)
            STACK_DMAS = 4 + 4 * TH
            NORM_STEPS = 14

            def real(n):
                return not isinstance(n, int) or 0 <= n < NQ

            def loads_of_parity(m, p):
                return 8 * (m - p) + 16

            def maxima_at(n, k):
                return (n + 1, 1, k - XLEAD) if k >= XLEAD else (n, 0, k + NSLOT - XLEAD)

            def tile_of_max(i):
                return i // 32, i % 32 // 8, i % 8 // 2, i % 2

            def run(eng, period):
                for n in range(-2, 2):
                    period(n, n % 2)
                with eng.Fori(1, NQ // 2 - 1) as i:
                    period(2 * i, 0)
                    period(2 * i + 1, 1)
                for n in range(NQ - 2, NQ + 2):
                    period(n, n % 2)

            with nc.Block() as block:
                @block.tensor
                def _(pe):
                    def scores(n, p, k):
                        th, j, h = k // 32, k % 32 // QH, k % QH
                        if j == 0 and h == 0:
                            pe.wait_ge(max_set, 16 * (2 * n + th + 1))
                        if counted(NSLOT * n + k - 1):
                            pe.wait_ge(exp_done, NSLOT * n + k - 1)
                        nc.tensor.matmul(s_bank[k % 2][:, :], k_st[p][0:KS, h, j * P:(j + 1) * P],
                                         q_st[p][0:KS, th, h, :], start=True, stop=True).then_inc(scores_ready, 1)

                    def scores_for_max(m, p, i):
                        th, h, tc, sh = tile_of_max(i)
                        if i == 0:
                            pe.wait_ge(stacked, 16 * STACK_DMAS * (m + 1))
                        if counted(NSLOT * m + i - 1):
                            pe.wait_ge(max_done, NSLOT * m + i - 1)
                        nc.tensor.matmul(x_bank[i % 2][:, :], q_st[p][0:KX, th, h, tc * P:(tc + 1) * P],
                                         k_st[p][0:KX, h, sh * HALF:(sh + 1) * HALF],
                                         start=True, stop=True).then_inc(x_ready, 1)

                    def times_v(m, p, c):
                        th, j = c // SJ, c % SJ
                        if c == 0:
                            pe.wait_ge(v_loaded[p], loads_of_parity(m, p))
                        if j == 0:
                            if counted(2 * m + th):
                                pe.wait_ge(o_copied, 2 * m + th)
                        pe.wait_ge(exp_done, NSLOT * m + QH * (c + 1))
                        for h in range(QH):
                            last = nc.tensor.matmul(o_bank[D * h:D * (h + 1), :], v_t[p][:, j, D * h:D * (h + 1)],
                                                    probs[:, c % PR, h, :], start=(j == 0), stop=(j == SJ - 1))
                        last.then_inc(pv_done, 1)

                    def denominators(m, r):
                        th, i = r // 4, r % 4
                        if i == 0:
                            if counted(2 * m + th):
                                pe.wait_ge(den_copied, 2 * m + th)
                        pe.wait_ge(pair_done, SJ * m + r + 1)
                        for h in range(QH):
                            last = nc.tensor.matmul(d_bank[D * h:D * (h + 1), :], ones[:, :], pair_sum[:, r % 2, h, :],
                                                    start=(i == 0), stop=(i == 3))
                        last.then_inc(den_done, 1)

                    def turn_max(m, th):
                        pe.wait_ge(negmax_done, 3 * (2 * m + th + 1))
                        if counted(2 * m + th):
                            pe.wait_ge(max_copied, 2 * m + th)
                        nc.tensor.matmul(m_bank[:, 0:P], neg_max[:, :], ident_r[:, :], start=True,
                                         stop=True).then_inc(max_turned, 1)

                    def turn_y8(m):
                        pe.wait_ge(norm_done, NORM_STEPS * (m + 1))
                        if counted(2 * m):
                            pe.wait_ge(ffn_added, 2 * m)
                        for kc in range(KC):
                            last = nc.tensor.transpose(f_bank_b[:, kc * P:(kc + 1) * P], y8[:, kc * P:(kc + 1) * P],
                                                       ident_b[:, :])
                        last.then_inc(y8_turned, 1)

                    def ffn(m, half, kc):
                        if kc == 0:
                            pe.wait_ge(y8_copied, m + 1)
                            pe.wait_ge(ffn_added, 2 * m + half)
                        last = nc.tensor.matmul(f_bank[:, :], y8_t[:, kc, :], w2q[:, kc, half * HALF:(half + 1) * HALF],
                                                start=(kc == 0), stop=(kc == KC - 1))
                        if kc == KC - 1:
                            last.then_inc(ffn_done, 1)

                    def period(n, p):
                        for k in range(NSLOT):
                            if real(n):
                                scores(n, p, k)
                            m, odd, i = maxima_at(n, k)
                            if real(m):
                                scores_for_max(m, (p + odd) % 2, i)
                            if k % 4 == 0:
                                if k >= 8 and real(n):
                                    times_v(n, p, (k - 8) // 4)
                                if k < 8 and real(n - 1):
                                    times_v(n - 1, 1 - p, 14 + k // 4)
                            if k % 8 == 2:
                                if k >= 18 and real(n):
                                    denominators(n, (k - 18) // 8)
                                if k < 18 and real(n - 1):
                                    denominators(n - 1, 6 + k // 8)
                            if k == 27 and real(n):
                                turn_max(n, 1)
                            if k == 59 and real(n + 1):
                                turn_max(n + 1, 0)
                            if k == 54 and real(n - 1):
                                turn_y8(n - 1)
                            if 2 <= k < 2 + KC and real(n - 2):
                                ffn(n - 2, 0, k - 2)
                            if 13 <= k < 13 + KC and real(n - 2):
                                ffn(n - 2, 1, k - 13)

                    run(pe, period)

                @block.scalar
                def _(act):
                    def exp(n, k):
                        c, h = k // QH, k % QH
                        if h == 0:
                            if counted(2 * SJ * n + c - PR + 1):
                                act.wait_ge(pv_done, 2 * SJ * n + c - PR + 1)
                            if counted(SJ * n + c // 2 - PR // 2 + 1):
                                act.wait_ge(pair_done, SJ * n + c // 2 - PR // 2 + 1)
                        act.wait_ge(scores_ready, NSLOT * n + k + 1)
                        nc.scalar.activation(probs[:, c % PR, h, :], s_bank[k % 2][:, :], ACT.Exp).then_inc(exp_done, 1)

                    def copy_o(m, th):
                        act.wait_ge(pv_done, 2 * SJ * m + SJ * (th + 1))
                        if counted(NORM_STEPS * (m - 1) + 1):
                            act.wait_ge(norm_done, NORM_STEPS * (m - 1) + 1)
                        nc.scalar.activation(o_raw[:, th], o_bank[:, :], ACT.Copy).then_inc(o_copied, 1)

                    def copy_den(m, th):
                        act.wait_ge(den_done, SJ * m + 4 * (th + 1))
                        if counted(16 * (2 * m + th)):
                            act.wait_ge(den_moved, 16 * (2 * m + th))
                        nc.scalar.activation(den[:, :], d_bank[:, :], ACT.Copy).then_inc(den_copied, 1)

                    def copy_max(m, th):
                        act.wait_ge(max_turned, 2 * m + th + 1)
                        if counted(16 * (2 * m + th)):
                            act.wait_ge(max_set, 16 * (2 * m + th))
                        nc.scalar.activation(max_rows[:, :], m_bank[0:2 * QH * TC, 0:P], ACT.Copy).then_inc(max_copied, 1)

                    def copy_y8(m):
                        act.wait_ge(y8_turned, m + 1)
                        if counted(2 * m):
                            act.wait_ge(ffn_done, 2 * m)
                        nc.scalar.activation(y8_t[:, :, :].rearrange("p k m -> p (k m)"), f_bank_b, ACT.Copy).then_inc(y8_copied, 1)

                    def period(n, p):
                        for k in range(NSLOT):
                            if real(n):
                                exp(n, k)
                            if k == 5 and real(n - 1):
                                copy_o(n - 1, 1)
                            if k == 12 and real(n - 1):
                                copy_den(n - 1, 1)
                            if k == 28 and real(n):
                                copy_max(n, 1)
                            if k == 37 and real(n):
                                copy_o(n, 0)
                            if k == 44 and real(n):
                                copy_den(n, 0)
                            if k == 55 and real(n - 1):
                                copy_y8(n - 1)
                            if k == 60 and real(n + 1):
                                copy_max(n + 1, 0)

                    run(act, period)

                @block.vector
                def _(dve):
                    def maximum(m, i):
                        th, h, tc, sh = tile_of_max(i)
                        if i % 32 == 0:
                            if counted(3 * (2 * m + th - 1)):
                                dve.wait_ge(negmax_done, 3 * (2 * m + th - 1))
                        dve.wait_ge(x_ready, NSLOT * m + i + 1)
                        at = h * TC + tc
                        nc.vector.tensor_reduce(part_max[:, th, sh, at:at + 1], x_bank[i % 2][:, :], AX,
                                                ALU.max).then_inc(max_done, 1)

                    def negate_max(m, th):
                        done = 3 * (2 * m + th)
                        dve.wait_ge(max_done, NSLOT * m + 32 * (th + 1))
                        if counted(done):
                            dve.wait_ge(negmax_done, done)
                        nc.vector.tensor_tensor(row_max[:, :], part_max[:, th, 0], part_max[:, th, 1], ALU.max).then_inc(negmax_done, 1)
                        dve.wait_ge(negmax_done, done + 1)
                        if counted(2 * m + th):
                            dve.wait_ge(max_turned, 2 * m + th)
                        R = QH * TC
                        nc.vector.tensor_scalar(neg_max[:, 0:R], row_max[:, :], -1.0, None, ALU.mult).then_inc(negmax_done, 1)
                        dve.wait_ge(negmax_done, done + 2)
                        nc.vector.scalar_tensor_tensor(neg_max[:, R:2 * R], row_max[:, :], -1.0, neg_max[:, 0:R].bitcast(F32),
                                                       ALU.mult, ALU.subtract).then_inc(negmax_done, 1)

                    def invert(m, th):
                        done = 2 * (2 * m + th)
                        dve.wait_ge(den_moved, 16 * (2 * m + th + 1))
                        if counted(16 * (2 * m + th)):
                            dve.wait_ge(inv_moved, 16 * (2 * m + th))
                        nc.vector.reciprocal(inv_c[:, :], den_c[:, :]).then_inc(inv_done, 1)
                        dve.wait_ge(inv_done, done + 1)
                        dve.wait_ge(tm_loaded, 16 * TH * (m + 1))
                        nc.vector.scalar_tensor_tensor(inv_c[:, :], inv_c[:, :], g1[:, 0:1], tm_c[:, th], ALU.mult,
                                                       ALU.mult).then_inc(inv_done, 1)

                    def norm(m, p, step):
                        x1 = res[p]
                        if step != 4:
                            if counted(NORM_STEPS * m + step):
                                dve.wait_ge(norm_done, NORM_STEPS * m + step)
                        if step == 0:
                            dve.wait_ge(o_copied, 2 * (m + 1))
                            dve.wait_ge(inv_spread, 16 * 2 * (m + 1))
                            ins = nc.vector.tensor_tensor(y[:, :], o_raw[:, :, :].rearrange("p a t -> p (a t)"),
                                                          inv_b[:, :, :].rearrange("p a t -> p (a t)"), ALU.mult)
                        elif step == 1:
                            dve.wait_ge(res_loaded[p], loads_of_parity(m, p))
                            ins = nc.vector.tensor_tensor(x1[:, :], x1[:, :], y[:, :], ALU.add)
                        elif step in (2, 3):
                            ins = nc.vector.bn_stats(st2[:, step - 2], x1[:, (step - 2) * HALF:(step - 1) * HALF])
                        elif step == 4:
                            ins = nc.vector.bn_aggr(mv2[:, :], st2[:, :, :])
                        elif step == 5:
                            if counted(m):
                                dve.wait_ge(rs2_done, m)
                            ins = nc.vector.tensor_scalar(ve2[:, :], mv2[:, 1:2], EPS, None, ALU.add)
                        elif step == 6:
                            dve.wait_ge(rs2_done, m + 1)
                            ins = nc.vector.tensor_tensor(rss[:, :], rs2[:, :], scl[:, :], ALU.mult)
                        elif step == 7:
                            ins = nc.vector.tensor_scalar(y[:, :], x1[:, :], mv2[:, 0:1], rss[:, 0:1], ALU.subtract, ALU.mult)
                        else:
                            if step == 11:
                                if counted(m):
                                    dve.wait_ge(y8_turned, m)
                            ins = f8_step(step - 8, y[:, :], big[:, :], y8[:, :], isnan[:, :])
                        ins.then_inc(norm_done, 1)

                    def add_ffn(m, p, half):
                        s = slice(half * HALF, (half + 1) * HALF)
                        dve.wait_ge(ffn_done, 2 * m + half + 1)
                        nc.vector.scalar_tensor_tensor(res[p][:, s], f_bank[:, :], g2[:, 0:1], res[p][:, s], ALU.mult,
                                                       ALU.add).then_inc(ffn_added, 1)

                    NORM_AT = {28: 0, 31: 1, 33: 2, 34: 3, 35: 4, 36: 5, 40: 6, 41: 7, 43: 8, 44: 9, 46: 10, 48: 11,
                               50: 12, 51: 13}

                    def period(n, p):
                        for k in range(NSLOT):
                            m, odd, i = maxima_at(n, k)
                            if NORM_AT.get(k) == 4 and real(n - 1):
                                dve.wait_ge(norm_done, NORM_STEPS * (n - 1) + 4)
                            if real(m):
                                maximum(m, i)
                            if k == 11 and real(n - 2):
                                add_ffn(n - 2, p, 0)
                            if k == 16 and real(n - 1):
                                invert(n - 1, 1)
                            if k == 22 and real(n - 2):
                                add_ffn(n - 2, p, 1)
                            if k == 23 and real(n):
                                negate_max(n, 1)
                            if k == 48 and real(n):
                                invert(n, 0)
                            if k == 55 and real(n + 1):
                                negate_max(n + 1, 0)
                            if k in NORM_AT and real(n - 1):
                                norm(n - 1, 1 - p, NORM_AT[k])

                    run(dve, period)

                @block.gpsimd
                def _(pool):
                    def add_pair(n, r):
                        pool.wait_ge(exp_done, NSLOT * n + 2 * QH * (r + 1))
                        if counted(SJ * n + r - 1):
                            pool.wait_ge(den_done, SJ * n + r - 1)
                        a = 2 * r % PR
                        nc.gpsimd.tensor_tensor(pair_sum[:, r % 2], probs[:, a], probs[:, a + 1], ALU.add).then_inc(pair_done, 1)

                    def period(n, p):
                        for r in range(SJ):
                            if real(n):
                                add_pair(n, r)
                            if r == 3 and real(n - 1):
                                pool.wait_ge(norm_done, NORM_STEPS * (n - 1) + 6)
                                nc.gpsimd.tensor_tensor(rs2[:, :], ve2[:, :], neg_half[:, 0:1], ALU.pow).then_inc(rs2_done, 1)

                    for i in range(2):
                        nc.gpsimd.memset(k_st[i][96:P, :, :].bitcast(F32), 1.0).then_inc(init_done, 1)
                        pool.wait_ge(init_done, i + 1)
                    nc.gpsimd.memset(neg_max[:, :].bitcast(F32), 0.0).then_inc(init_done, 1)
                    run(pool, period)

                @block.sync
                def _(sp):
                    qx_q = qx_scr.rearrange("r b q t -> r (b q) t")
                    kx_q = kx_scr.rearrange("r b q t -> r (b q) t")
                    tm_q = tm_scr.rearrange("b q t -> (b q) t")

                    def stack(m, p):
                        if counted(NSLOT * (m - 1)):
                            sp.wait_ge(scores_ready, NSLOT * (m - 1))
                        if counted(NSLOT * (m - 1)):
                            sp.wait_ge(x_ready, NSLOT * (m - 1))
                        rows = bass.ds(m * P, P)
                        k_part = [k_scr[part, rows, :].rearrange("(h d) s -> d h s", d=D) for part in range(2)]
                        q_part = [q_scr[part, rows, :].rearrange("(h d) (a t) -> d a h t", d=D, a=TH) for part in range(2)]
                        for at, part in ((0, 0), (D, 1), (2 * D, 0)):
                            sp.dma_start(k_st[p][at:at + D, :, :].bitcast(F32), k_part[part]).then_inc(stacked, 16)
                        sp.dma_start(k_st[p][96:98, :, :].bitcast(F32), kx_q[:, bass.ds(m, 1), :].broadcast_to((2, QH, S))).then_inc(stacked, 16)
                        for at, part in ((0, 0), (D, 0), (2 * D, 1)):
                            for th in range(TH):
                                sp.dma_start(q_st[p][at:at + D, th, :, :].bitcast(F32), q_part[part][:, th]).then_inc(stacked, 16)
                        for th in range(TH):
                            row = qx_q[:, bass.ds(m, 1), th * HALF:(th + 1) * HALF]
                            sp.dma_start(q_st[p][96:98, th, :, :].bitcast(F32), row.broadcast_to((2, QH, HALF))).then_inc(stacked, 16)

                    def load_v(m, p):
                        if counted(2 * SJ * (m - 1)):
                            sp.wait_ge(pv_done, 2 * SJ * (m - 1))
                        sp.dma_start(v_t[p][:, :, :], v_scr[bass.ds(m, 1), :, :].rearrange("o (j s) d -> s (o j) d", s=P)).then_inc(v_loaded[p], 16)

                    def move_den(m, th):
                        sp.wait_ge(den_copied, 2 * m + th + 1)
                        sp.dma_start(den_c[:, :], den[0:P:D, :]).then_inc(den_moved, 16)

                    def move_inv(m, th):
                        sp.wait_ge(inv_done, 2 * (2 * m + th + 1))
                        sp.dma_start(inv_scr[th].rearrange("h (u v) -> (h u) v", u=D), inv_c[:, :]).then_inc(inv_moved, 16)
                        sp.wait_ge(inv_moved, 16 * (2 * m + th + 1))
                        if counted(NORM_STEPS * (m - 1) + 1):
                            sp.wait_ge(norm_done, NORM_STEPS * (m - 1) + 1)
                        sp.dma_start(inv_b[:, th, :], inv_scr[th].unsqueeze(1).broadcast_to((QH, D, HALF))).then_inc(inv_spread, 16)

                    def load_tm(m):
                        if counted(16 * 2 * m):
                            sp.wait_ge(inv_spread, 16 * 2 * m)
                        for th in range(TH):
                            row = tm_q[bass.ds(m, 1), th * HALF:(th + 1) * HALF]
                            sp.dma_start(tm_c[:, th, :], row.broadcast_to((QH, HALF))).then_inc(tm_loaded, 16)

                    def set_max(m, th, p):
                        sp.wait_ge(max_copied, 2 * m + th + 1)
                        sp.dma_start(q_st[p][KX:KS, th, :, :].bitcast(F32), max_rows[:, :].bitcast(F32)).then_inc(max_set, 16)

                    def load_res(m, p):
                        if counted(16 * (m - 1)):
                            sp.wait_ge(out_stored, 16 * (m - 1))
                        sp.dma_start(res[p][:, :], x_rows[bass.ds(m * P, P), :]).then_inc(res_loaded[p], 16)

                    def store(m, p):
                        sp.wait_ge(ffn_added, 2 * (m + 1))
                        sp.dma_start(out_rows[bass.ds(m * P, P), :], res[p][:, :]).then_inc(out_stored, 16)

                    def period(n, p):
                        if real(n + 1):
                            stack(n + 1, 1 - p)
                            load_v(n + 1, 1 - p)
                        if real(n - 1):
                            move_den(n - 1, 1)
                            move_inv(n - 1, 1)
                        if real(n):
                            load_tm(n)
                        if real(n - 2):
                            store(n - 2, p)
                        if real(n):
                            set_max(n, 1, p)
                            load_res(n, p)
                            move_den(n, 0)
                            move_inv(n, 0)
                        if real(n + 1):
                            set_max(n + 1, 0, 1 - p)

                    sp.wait_ge(init_done, 3)
                    run(sp, period)
                    sp.wait_ge(out_stored, 16 * NQ)


_INS = ['x', 'ctx_2048', 'mask_Bx1x2048_fk1', 'g_xattn', 'g_ffn', 'L0_xattn_Wq', 'L0_xattn_bq', 'L0_xattn_Wk',
        'L0_xattn_bk', 'L0_xattn_Wv', 'L0_xattn_bv', 'L0_ffn_input2', 'L0_ffn_scale', 'L0_ffn_scale1']


def kernel(**inputs):
    import numpy as _np
    import concourse.bacc as _bacc
    from concourse import mybir as _mybir
    from concourse.bass_utils import run_bass_kernel_spmd as _run

    nc = _bacc.Bacc("TRN2", target_bir_lowering=False, num_devices=1)
    arrays, args = {}, []
    for name in _INS:
        a = _np.ascontiguousarray(inputs[name])
        arrays[f"in_{name}_dram"] = a
        args.append(nc.dram_tensor(f"in_{name}_dram", a.shape, _mybir.dt.from_np(a.dtype), kind="ExternalInput").ap())
    shape = arrays["in_x_dram"].shape
    args.append(nc.dram_tensor("out_0_dram", shape, _mybir.dt.float32, kind="ExternalOutput").ap())
    flamingo_gated_layer(nc, *args)
    r = _run(nc, [arrays], core_ids=[0])
    return r.results[0]["out_0_dram"]
```

```python
from contextlib import ExitStack

import concourse.bass as bass
from concourse import mybir

ALU = mybir.AluOpType
ACT = mybir.ActivationFunctionType
AX = mybir.AxisListType.X
F32 = mybir.dt.float32
F32R = mybir.dt.float32r
BF16 = mybir.dt.bfloat16
U32 = mybir.dt.uint32

P = 128
HALF = 512
EPS = 1e-5

NEG_Q, NEG_K = 8000.0, 125.0

EXPONENT_BITS = 0x7F800000
F8_MIN_NORMAL = 2.0 ** -6
ROUND_TO_4_BITS = 1.5 * 2.0 ** 20
F8_OVERFLOW = 2.0 ** 120 / 1.8


def counted(value):
    return not isinstance(value, int) or value > 0


def flamingo_gated_layer(nc, x, ctx, mask, g_xattn, g_ffn, Wq, bq, Wk, bk, Wv, bv, W2, scale, scale1, out):
    B, C, T = x.shape
    S = ctx.shape[2]
    HEADS, D = 16, C // 16
    CB = C // P
    QH = P // D
    QUADS = C // P
    NQ = B * QUADS
    SJ = S // P
    TH = T // HALF
    TC = HALF // P
    KC = T // P
    INV_SQRT_D = 1.0 / float(D) ** 0.5
    assert (C, T, S, D, TH) == (512, 1024, 1024, 32, 2)

    x_rows = x.rearrange("b c t -> (b c) t")
    out_rows = out.rearrange("b c t -> (b c) t")

    q_scr = nc.dram_tensor("q_scr", [2, B * C, T], F32, kind="Internal").ap()
    k_scr = nc.dram_tensor("k_scr", [2, B * C, S], F32, kind="Internal").ap()
    v_scr = nc.dram_tensor("v_scr", [NQ, S, P], F32, kind="Internal").ap()
    inv_scr = nc.dram_tensor("inv_scr", [TH, QH, HALF], F32, kind="Internal").ap()
    qx_scr = nc.dram_tensor("qx_scr", [2, B, QUADS, T], F32, kind="Internal").ap()
    kx_scr = nc.dram_tensor("kx_scr", [4, B, QUADS, S], F32, kind="Internal").ap()
    tm_scr = nc.dram_tensor("tm_scr", [B, QUADS, T], F32, kind="Internal").ap()

    ctxs = ExitStack()
    with ctxs:
        def sem(name, stack=ctxs):
            return stack.enter_context(nc.semaphore(name))

        def sb(name, shape, dt, stack=ctxs):
            return stack.enter_context(nc.sbuf_tensor(name, shape, dt))

        def pb(name, shape, dt, stack=ctxs):
            return stack.enter_context(nc.psum_tensor(name, shape, dt))

        ident_r = sb("ident_r", [P, P], F32R)
        ident_b = sb("ident_b", [P, P], BF16)
        ones = sb("ones", [P, D], F32)
        neg_half = sb("neg_half", [P, CB], F32)
        w2q = sb("w2q", [P, KC, T], BF16)
        g1 = sb("g1", [P, 1], F32)
        g2 = sb("g2", [P, 1], F32)
        scl = sb("scl", [P, 1], F32)
        scl1 = sb("scl1", [P, 1], F32)

        F8_STEPS = 6

        def f8_step(step, y, big, q, isnan):
            if step == 0:
                return nc.vector.tensor_scalar(big.bitcast(U32), y.bitcast(U32), EXPONENT_BITS, None, ALU.bitwise_and)
            if step == 1:
                return nc.vector.tensor_scalar(big, big, F8_MIN_NORMAL, ROUND_TO_4_BITS, ALU.max, ALU.mult)
            if step == 2:
                return nc.vector.tensor_tensor(y, y, big, ALU.add)
            if step == 3:
                return nc.vector.tensor_tensor(q, y, big, ALU.subtract)
            if step == 4:
                return nc.vector.tensor_scalar(isnan, q, F8_OVERFLOW, 0.0, ALU.mult, ALU.mult)
            return nc.vector.tensor_tensor(q, q, isnan, ALU.add)

        with ExitStack() as st:
            w_names = ("k", "v", "q")
            w_hi = {w: sb(f"w_hi_{w}", [P, CB, C], F32R, st) for w in w_names}
            w_lo = {w: sb(f"w_lo_{w}", [P, CB, C], F32R, st) for w in w_names}
            bias_q = sb("bias_q", [P, CB], F32, st)
            bias_k = sb("bias_k", [P, CB], F32, st)
            bias_v = sb("bias_v", [P, C], F32, st)
            sm_cols = sb("sm_cols", [P, B * SJ], F32, st)
            bank = [pb(f"bank{i}", [P, HALF], F32, st) for i in range(8)]
            c_raw = sb("c_raw", [P, CB, S], F32, st)
            x_raw = sb("x_raw", [P, CB, T], F32, st)
            c_loaded = [sem(f"c_loaded{i}", st) for i in range(CB)]
            x_loaded = [sem(f"x_loaded{i}", st) for i in range(CB)]

            with ExitStack() as su:
                w_nat = sb("w_nat", [P, 3, CB, C], F32, su)
                m_nat = sb("m_nat", [B * SJ, P], F32, su)
                m_rows = sb("m_rows", [B, T], F32, su)
                qx = sb("qx", [B, 2, T], F32R, su)
                kx = sb("kx", [B, 3, S], F32R, su)
                ident_f = sb("ident_f", [P, P], F32, su)
                gl = sb("gl", [P, 4], F32, su)
                gt = sb("gt", [P, 4], F32, su)
                w_loaded = [sem(f"w_loaded{i}", su) for i in range(3)]
                bias_loaded = sem("bias_loaded", su)
                mask_loaded = sem("mask_loaded", su)
                gates_loaded = sem("gates_loaded", su)
                ident_done = sem("ident_done", su)
                w_turned = sem("w_turned", su)
                hi_done = sem("hi_done", su)
                lo_done = sem("lo_done", su)
                m_turned = sem("m_turned", su)
                tanh_done = sem("tanh_done", su)
                chain_done = sem("setup_chain", su)
                extra_done = sem("extra_done", su)
                stored = sem("setup_stored", su)

                with nc.Block() as block:
                    @block.sync
                    def _(sp):
                        sp.dma_start(m_nat[:, :], mask.rearrange("b o (j p) -> (b o j) p", p=P)).then_inc(mask_loaded, 16)
                        sp.dma_start(m_rows[:, :], mask.rearrange("b o t -> (b o) t")).then_inc(mask_loaded, 16)
                        for n, w in enumerate((Wk, Wv, Wq)):
                            sp.dma_start(w_nat[:, n], w.rearrange("(a p) c -> p a c", p=P)).then_inc(w_loaded[n], 16)
                        sp.wait_ge(extra_done, 4)
                        for q in range(QUADS):
                            for r in range(2):
                                sp.dma_start(qx_scr[r, :, q, :], qx[:, r, :].bitcast(F32)).then_inc(stored, 16)
                            for r in range(4):
                                sp.dma_start(kx_scr[r, :, q, :], kx[:, min(r, 2), :].bitcast(F32)).then_inc(stored, 16)
                        for q in range(QUADS):
                            sp.dma_start(tm_scr[:, q, :], m_rows[:, :]).then_inc(stored, 16)
                        sp.wait_ge(stored, 16 * 7 * QUADS)

                    @block.gpsimd
                    def _(pool):
                        pool.memset(ident_f[:, :], 0.0).then_inc(ident_done, 1)
                        pool.wait_ge(ident_done, 1)
                        pool.affine_select(out=ident_f[:, :], in_=ident_f[:, :], compare_op=ALU.not_equal, fill=1.0,
                                           base=0, pattern=[[-1, P]], channel_multiplier=1).then_inc(ident_done, 1)
                        pool.memset(ones[:, :], 1.0).then_inc(ident_done, 1)
                        pool.memset(neg_half[:, :], -0.5).then_inc(ident_done, 1)

                    @block.scalar
                    def _(act):
                        act.dma_start(bias_k[:, :], bk.rearrange("(a p) -> p a", p=P), allow_slow_non_contiguous=True).then_inc(bias_loaded, 16)
                        act.dma_start(bias_q[:, :], bq.rearrange("(a p) -> p a", p=P), allow_slow_non_contiguous=True).then_inc(bias_loaded, 16)
                        act.dma_start(bias_v[:, :], bv.partition_broadcast(P)).then_inc(bias_loaded, 16)
                        for n, g in enumerate((g_xattn, g_ffn, scale, scale1)):
                            act.dma_start(gl[:, n:n + 1], g.partition_broadcast(P)).then_inc(gates_loaded, 16)
                        for cb in range(CB):
                            act.dma_start(c_raw[:, cb], ctx[0, cb * P:(cb + 1) * P, :]).then_inc(c_loaded[cb], 16)
                        for cb in range(CB):
                            act.dma_start(x_raw[:, cb], x[0, cb * P:(cb + 1) * P, :]).then_inc(x_loaded[cb], 16)
                        for n, w in enumerate(w_names):
                            for cb in range(CB):
                                i = n * CB + cb
                                act.wait_ge(w_turned, i + 1)
                                act.activation(w_hi[w][:, cb], bank[i % 6][:, :], ACT.Copy).then_inc(hi_done, 1)
                        act.wait_ge(gates_loaded, 64)
                        act.activation(gt[:, 0:2], gl[:, 0:2], ACT.Tanh).then_inc(tanh_done, 1)
                        act.wait_ge(bias_loaded, 48)

                    @block.tensor
                    def _(pe):
                        pe.wait_ge(ident_done, 2)
                        for n in range(3):
                            pe.wait_ge(w_loaded[n], 16)
                            for cb in range(CB):
                                i = n * CB + cb
                                if counted(i - 5):
                                    pe.wait_ge(lo_done, i - 5)
                                for ob in range(CB):
                                    last = nc.tensor.transpose(bank[i % 6][:, ob * P:(ob + 1) * P],
                                                               w_nat[:, n, ob, cb * P:(cb + 1) * P], ident_f[:, :])
                                last.then_inc(w_turned, 1)
                        pe.wait_ge(mask_loaded, 32)
                        nc.tensor.transpose(bank[7][:, 0:B * SJ], m_nat[:, :], ident_f[0:B * SJ, 0:B * SJ]).then_inc(m_turned, 1)

                    @block.vector
                    def _(dve):
                        n_chain = [0]

                        def chain(ins):
                            n_chain[0] += 1
                            ins.then_inc(chain_done, 1)
                            dve.wait_ge(chain_done, n_chain[0])

                        dve.wait_ge(ident_done, 2)
                        chain(nc.vector.tensor_copy(ident_r[:, :], ident_f[:, :]))
                        chain(nc.vector.tensor_copy(ident_b[:, :], ident_f[:, :]))
                        dve.wait_ge(mask_loaded, 32)
                        chain(nc.vector.tensor_scalar(qx[:, 0, :], m_rows[:, :], -NEG_Q, None, ALU.mult))
                        nc.vector.tensor_scalar(qx[:, 1, :], m_rows[:, :], 1.0, NEG_Q, ALU.subtract, ALU.mult).then_inc(extra_done, 1)
                        nc.vector.tensor_scalar(kx[:, 0, :], m_rows[:, :], 1.0, -NEG_K, ALU.subtract, ALU.mult).then_inc(extra_done, 1)
                        nc.vector.tensor_scalar(kx[:, 1, :], m_rows[:, :], 0.0, NEG_K, ALU.mult, ALU.add).then_inc(extra_done, 1)
                        nc.vector.tensor_scalar(kx[:, 2, :], m_rows[:, :], 0.0, 1.0, ALU.mult, ALU.add).then_inc(extra_done, 1)
                        for n, w in enumerate(w_names):
                            for cb in range(CB):
                                i = n * CB + cb
                                dve.wait_ge(hi_done, i + 1)
                                nc.vector.tensor_tensor(w_lo[w][:, cb], bank[i % 6][:, :], w_hi[w][:, cb].bitcast(F32),
                                                        ALU.subtract).then_inc(lo_done, 1)
                        dve.wait_ge(m_turned, 1)
                        chain(nc.vector.tensor_copy(sm_cols[:, :], bank[7][:, 0:B * SJ]))
                        dve.wait_ge(tanh_done, 1)
                        chain(nc.vector.tensor_copy(g1[:, :], gt[:, 0:1]))
                        chain(nc.vector.tensor_copy(scl[:, :], gl[:, 2:3]))
                        chain(nc.vector.tensor_copy(scl1[:, :], gl[:, 3:4]))
                        chain(nc.vector.reciprocal(gt[:, 2:4], gl[:, 2:4]))
                        chain(nc.vector.tensor_tensor(gt[:, 2:3], gt[:, 2:3], gt[:, 3:4], ALU.mult))
                        chain(nc.vector.tensor_tensor(g2[:, :], gt[:, 1:2], gt[:, 2:3], ALU.mult))

            with ExitStack() as pr:
                c_hi = sb("c_hi", [P, CB, S], F32R, pr)
                c_lo = sb("c_lo", [P, CB, S], F32R, pr)
                xn = x_raw
                x_hi = sb("x_hi", [P, CB, T], F32R, pr)
                x_lo = sb("x_lo", [P, CB, T], F32R, pr)
                m_b = sb("m_b", [P, T], F32, pr)
                m_bs = sb("m_bs", [P, T], F32, pr)
                stats = sb("stats", [P, CB, 2, 6], F32, pr)
                mv = sb("mv", [P, CB, 2], F32, pr)
                sm_now = sb("sm_now", [P, SJ], F32, pr)
                credit = sb("credit", [P, 1], F32, pr)
                W2B = KC // B
                w2f = sb("w2f", [P, W2B, T], F32, pr)
                w2big = sb("w2big", [P, T], F32, pr)
                w2nan = sb("w2nan", [P, T], BF16, pr)
                w2_loaded = sem("w2_loaded", pr)
                w2_chain = sem("w2_chain", pr)
                w2_done = sem("w2_done", pr)
                ve = sb("ve", [P, CB], F32, pr)
                rstd = sb("rstd", [P, CB], F32, pr)
                STG = 4
                stage = sb("stage", [P, STG, HALF], F32, pr)
                stage_hi = sb("stage_hi", [P, STG, HALF], F32R, pr)
                stage_lo = sb("stage_lo", [P, STG, HALF], F32R, pr)
                m_loaded = sem("m_loaded", pr)
                chi_done = sem("chi_done", pr)
                clo_done = sem("clo_done", pr)
                xhi_done = sem("xhi_done", pr)
                xlo_done = sem("xlo_done", pr)
                xn_done = sem("xn_done", pr)
                stats_done = sem("stats_done", pr)
                ve_done = sem("ve_done", pr)
                rstd_done = sem("rstd_done", pr)
                sm_set = sem("sm_set", pr)
                mbs_done = sem("mbs_done", pr)
                group_done = sem("group_done", pr)
                evacuated = sem("evacuated", pr)
                v_masked = sem("v_masked", pr)
                v_stored = [sem(f"v_stored{i}", pr) for i in range(STG)]
                qk_hi = sem("qk_hi", pr)
                qk_lo = sem("qk_lo", pr)
                qk_stored = [sem(f"qk_stored{i}", pr) for i in range(STG)]
                NB = len(bank)
                GK = CB * 2
                GV = SJ
                G = 2 * GK + GV

                def run(eng, batch):
                    batch(0, True)
                    if B > 2:
                        with eng.Fori(1, B - 1) as b:
                            batch(b, True)
                    batch(B - 1, False)

                with nc.Block() as block:
                    @block.gpsimd
                    def _(pool):
                        def invert_std(b):
                            pool.wait_ge(ve_done, b + 1)
                            nc.gpsimd.tensor_tensor(rstd[:, :], ve[:, :], neg_half[:, :], ALU.pow).then_inc(rstd_done, 1)

                        def batch(b, more):
                            for e in range(2 * GK):
                                if e == GK and more:
                                    invert_std(b + 1)
                                pool.wait_ge(qk_hi, b * 2 * GK + e + 1)
                                if counted(32 * (b * (2 * GK // STG) + e // STG)):
                                    pool.wait_ge(qk_stored[e % STG], 32 * (b * (2 * GK // STG) + e // STG))
                                g = e if e < GK else e + GV
                                nc.gpsimd.tensor_tensor(stage_lo[:, e % STG], stage[:, g % STG], stage_hi[:, e % STG].bitcast(F32),
                                                        ALU.subtract).then_inc(qk_lo, 1)

                        invert_std(0)
                        run(pool, batch)

                    @block.sync
                    def _(sp):
                        def load_mask(b):
                            sp.dma_start(m_b[:, :], mask[b, 0, :].partition_broadcast(P)).then_inc(m_loaded, 16)

                        def batch(b, more):
                            for g in range(G):
                                if g == GK and more:
                                    sp.wait_ge(evacuated, b * G + GK)
                                    load_mask(b + 1)
                                if GK <= g < GK + GV:
                                    j = g - GK
                                    sp.wait_ge(v_masked, b * GV + j + 1)
                                    dst = v_scr[bass.ds(b * QUADS, QUADS), j * P:(j + 1) * P, :].rearrange("q s d -> s q d")
                                    src = stage[:, g % STG].rearrange("p (q d) -> p q d", q=QUADS)
                                    sp.dma_start(dst, src).then_inc(v_stored[g % STG], 16)
                                    continue
                                to, gg, e = (k_scr, g, g) if g < GK else (q_scr, g - GK - GV, g - GV)
                                s = slice((gg % 2) * HALF, (gg % 2 + 1) * HALF)
                                sp.wait_ge(qk_lo, b * 2 * GK + e + 1)
                                for part, src in ((0, stage_hi), (1, stage_lo)):
                                    sp.dma_start(to[part, bass.ds(b * C + (gg // 2) * P, P), s],
                                                 src[:, e % STG].bitcast(F32)).then_inc(qk_stored[e % STG], 16)

                        load_mask(0)
                        run(sp, batch)
                        for i in range(STG):
                            sp.wait_ge(v_stored[i], 16 * B * (GV // STG))
                            sp.wait_ge(qk_stored[i], 32 * B * (2 * GK // STG))

                    @block.scalar
                    def _(act):
                        def load_ctx(b):
                            act.wait_ge(clo_done, b * CB)
                            for cb in range(CB):
                                act.dma_start(c_raw[:, cb], ctx[b, cb * P:(cb + 1) * P, :]).then_inc(c_loaded[cb], 16)

                        def load_x(b):
                            act.wait_ge(xlo_done, b * CB)
                            for cb in range(CB):
                                act.dma_start(x_raw[:, cb], x[b, cb * P:(cb + 1) * P, :]).then_inc(x_loaded[cb], 16)

                        def load_w2(b):
                            if counted(b):
                                act.wait_ge(w2_done, b)
                            act.dma_start(w2f[:, :, :], W2[bass.ds(b * (W2B * P), W2B * P), :].rearrange("(a p) n -> p a n", p=P)).then_inc(w2_loaded, 16)

                        def split_ctx(b):
                            if counted(b * G - GK):
                                act.wait_ge(group_done, b * G - GK)
                            for cb in range(CB):
                                act.wait_ge(c_loaded[cb], 16 * (b + 1))
                                nc.scalar.activation(c_hi[:, cb], c_raw[:, cb], ACT.Copy).then_inc(chi_done, 1)

                        def high(b, g):
                            e = g if g < GK else g - GV
                            act.wait_ge(evacuated, b * G + g + 1)
                            if counted(32 * (b * (2 * GK // STG) + e // STG)):
                                act.wait_ge(qk_stored[e % STG], 32 * (b * (2 * GK // STG) + e // STG))
                            nc.scalar.activation(stage_hi[:, e % STG], stage[:, g % STG], ACT.Copy).then_inc(qk_hi, 1)

                        def batch(b, more):
                            if more:
                                load_ctx(b + 1)
                            if counted(b * G):
                                act.wait_ge(group_done, b * G)
                            for cb in range(CB):
                                act.wait_ge(xn_done, b * CB + cb + 1)
                                nc.scalar.activation(x_hi[:, cb], xn[:, cb], ACT.Copy).then_inc(xhi_done, 1)
                            for g in range(GK):
                                high(b, g)
                            for g in range(GK, GK + GV):
                                j = g - GK
                                act.wait_ge(evacuated, b * G + g + 1)
                                nc.scalar.activation(stage[:, g % STG], stage[:, g % STG], ACT.Copy,
                                                     scale=sm_now[:, j:j + 1]).then_inc(v_masked, 1)
                            if more:
                                load_x(b + 1)
                                load_w2(b + 1)
                                split_ctx(b + 1)
                            for g in range(GK + GV, G):
                                high(b, g)

                        load_w2(0)
                        split_ctx(0)
                        run(act, batch)

                    @block.tensor
                    def _(pe):
                        def batch(b, more):
                            for g in range(G):
                                ready, hi, lo = (clo_done, c_hi, c_lo) if g < GK + GV else (xlo_done, x_hi, x_lo)
                                if counted(b * G + g + 1 - NB):
                                    pe.wait_ge(evacuated, b * G + g + 1 - NB)
                                acc = bank[g % NB][:, :]
                                for cb in range(CB):
                                    if g in (0, GK + GV):
                                        pe.wait_ge(ready, b * CB + cb + 1)
                                    if GK <= g < GK + GV:
                                        j = g - GK
                                        s = slice(j * P, (j + 1) * P)
                                        pairs = ((hi[:, cb, s], w_hi["v"][:, cb]), (lo[:, cb, s], w_hi["v"][:, cb]),
                                                 (hi[:, cb, s], w_lo["v"][:, cb]))
                                    else:
                                        w, gg = ("k", g) if g < GK else ("q", g - GK - GV)
                                        o = slice((gg // 2) * P, (gg // 2 + 1) * P)
                                        s = slice((gg % 2) * HALF, (gg % 2 + 1) * HALF)
                                        pairs = ((w_hi[w][:, cb, o], hi[:, cb, s]), (w_lo[w][:, cb, o], hi[:, cb, s]),
                                                 (w_hi[w][:, cb, o], lo[:, cb, s]))
                                    for n, (a, m) in enumerate(pairs):
                                        last = nc.tensor.matmul(acc, a, m, start=(cb == 0 and n == 0),
                                                                stop=(cb == CB - 1 and n == 2))
                                last.then_inc(group_done, 1)

                        run(pe, batch)

                    @block.vector
                    def _(dve):
                        def low_ctx(b):
                            for cb in range(CB):
                                dve.wait_ge(chi_done, b * CB + cb + 1)
                                nc.vector.tensor_tensor(c_lo[:, cb], c_raw[:, cb], c_hi[:, cb].bitcast(F32),
                                                        ALU.subtract).then_inc(clo_done, 1)

                        def evacuate(b, g):
                            dve.wait_ge(group_done, b * G + g + 1)
                            if GK <= g - STG < GK + GV:
                                dve.wait_ge(v_stored[g % STG], 16 * (b * (GV // STG) + (g - STG - GK) // STG + 1))
                            else:
                                if counted(b * 2 * GK + (g - STG if g < GK + STG else g - STG - GV) + 1):
                                    dve.wait_ge(qk_lo, b * 2 * GK + (g - STG if g < GK + STG else g - STG - GV) + 1)
                            acc, to = bank[g % NB][:, :], stage[:, g % STG]
                            if GK <= g < GK + GV:
                                nc.vector.tensor_tensor(to, acc, bias_v[:, :], ALU.add).then_inc(evacuated, 1)
                            else:
                                bias, m, gg = (bias_k, m_b, g) if g < GK else (bias_q, m_bs, g - GK - GV)
                                s = slice((gg % 2) * HALF, (gg % 2 + 1) * HALF)
                                nc.vector.scalar_tensor_tensor(to, acc, bias[:, gg // 2:gg // 2 + 1], m[:, s],
                                                               ALU.add, ALU.mult).then_inc(evacuated, 1)

                        def round_w2(b):
                            dve.wait_ge(w2_loaded, 16 * (b + 1))
                            for a in range(W2B):
                                wf = w2f[:, a]
                                q = w2q[:, bass.ds(b * W2B + a, 1), :].rearrange("p a n -> p (a n)")
                                done = (b * W2B + a) * (F8_STEPS + 1)
                                nc.vector.tensor_scalar(wf, wf, scl1[:, 0:1], None, ALU.mult).then_inc(w2_chain, 1)
                                for step in range(F8_STEPS):
                                    dve.wait_ge(w2_chain, done + step + 1)
                                    f8_step(step, wf, w2big[:, :], q, w2nan[:, :]).then_inc(w2_chain, 1)
                                dve.wait_ge(w2_chain, done + F8_STEPS + 1)
                            nc.vector.memset(credit[:, :], 0.0).then_inc(w2_done, 1)

                        def statistics(b):
                            for cb in range(CB):
                                dve.wait_ge(x_loaded[cb], 16 * (b + 1))
                                for h in range(2):
                                    nc.vector.bn_stats(stats[:, cb, h], x_raw[:, cb, h * HALF:(h + 1) * HALF]).then_inc(stats_done, 1)
                            if counted(b * GV):
                                dve.wait_ge(v_masked, b * GV)
                            dve.wait_ge(stats_done, 3 * CB * b + 2 * CB)
                            nc.vector.tensor_copy(sm_now[:, :], sm_cols[:, bass.ds(b * SJ, SJ)]).then_inc(sm_set, 1)
                            for cb in range(CB):
                                nc.vector.bn_aggr(mv[:, cb], stats[:, cb]).then_inc(stats_done, 1)
                            dve.wait_ge(stats_done, 3 * CB * (b + 1))
                            nc.vector.tensor_scalar(ve[:, :], mv[:, :, 1], EPS, None, ALU.add).then_inc(ve_done, 1)

                        def normalize(b):
                            dve.wait_ge(rstd_done, b + 1)
                            for cb in range(CB):
                                nc.vector.tensor_scalar(xn[:, cb], x_raw[:, cb], mv[:, cb, 0:1], rstd[:, cb:cb + 1],
                                                        ALU.subtract, ALU.mult).then_inc(xn_done, 1)

                        def batch(b, more):
                            dve.wait_ge(m_loaded, 16 * (b + 1))
                            if counted(b * G):
                                dve.wait_ge(evacuated, b * G)
                            nc.vector.tensor_scalar(m_bs[:, :], m_b[:, :], INV_SQRT_D, None, ALU.mult).then_inc(mbs_done, 1)
                            for g in range(GK // 2):
                                evacuate(b, g)
                            for cb in range(CB):
                                dve.wait_ge(xhi_done, b * CB + cb + 1)
                                nc.vector.tensor_tensor(x_lo[:, cb], xn[:, cb], x_hi[:, cb].bitcast(F32),
                                                        ALU.subtract).then_inc(xlo_done, 1)
                            for g in range(GK // 2, GK + GV // 2):
                                evacuate(b, g)
                            round_w2(b)
                            for g in range(GK + GV // 2, GK + GV):
                                evacuate(b, g)
                            if more:
                                statistics(b + 1)
                                low_ctx(b + 1)
                            dve.wait_ge(mbs_done, b + 1)
                            for g in range(GK + GV, G):
                                if g == G - GK // 2 and more:
                                    normalize(b + 1)
                                evacuate(b, g)

                        low_ctx(0)
                        statistics(0)
                        normalize(0)
                        run(dve, batch)

        with ExitStack() as at:
            NSLOT = 2 * SJ * QH
            KX, KS = 98, 100
            PR = 4
            XLEAD = 19

            k_st = [sb(f"k_st{i}", [P, QH, S], F32R, at) for i in range(2)]
            q_st = [sb(f"q_st{i}", [P, TH, QH, HALF], F32R, at) for i in range(2)]
            probs = sb("probs", [P, PR, QH, HALF], F32, at)
            pair_sum = sb("pair_sum", [P, 2, QH, HALF], F32, at)
            v_t = [sb(f"v_t{i}", [P, SJ, P], F32, at) for i in range(2)]
            part_max = sb("part_max", [P, TH, 2, QH * TC], F32, at)
            row_max = sb("row_max", [P, QH * TC], F32, at)
            neg_max = sb("neg_max", [P, P], F32R, at)
            max_rows = sb("max_rows", [2 * QH * TC, P], F32R, at)
            o_raw = sb("o_raw", [P, TH, HALF], F32, at)
            den = sb("den", [P, HALF], F32, at)
            den_c = sb("den_c", [P, HALF // 32], F32, at)
            inv_c = sb("inv_c", [P, HALF // 32], F32, at)
            tm_c = sb("tm_c", [P, TH, HALF // 32], F32, at)
            inv_b = sb("inv_b", [P, TH, HALF], F32, at)
            res = [sb(f"res{i}", [P, T], F32, at) for i in range(2)]
            y = sb("y", [P, T], F32, at)
            big = sb("big", [P, T], F32, at)
            y8 = sb("y8", [P, T], BF16, at)
            isnan = sb("isnan", [P, T], BF16, at)
            y8_t = sb("y8_t", [P, KC, P], BF16, at)
            st2 = sb("st2", [P, 2, 6], F32, at)
            mv2 = sb("mv2", [P, 2], F32, at)
            ve2 = sb("ve2", [P, 1], F32, at)
            rs2 = sb("rs2", [P, 1], F32, at)
            rss = sb("rss", [P, 1], F32, at)

            s_bank = [pb(f"s_bank{i}", [P, HALF], F32, at) for i in range(2)]
            XB = 3
            x_bank = [pb(f"x_bank{i}", [P, HALF], F32, at) for i in range(XB)]
            o_bank = pb("o_bank", [P, HALF], F32, at)
            d_bank = pb("d_bank", [P, HALF], F32, at)
            f_bank = pb("f_bank", [P, HALF], F32, at)
            f_bank_b = f_bank[:, :].bitcast(BF16)

            init_done = sem("init_done", at)
            stacked = sem("stacked", at)
            v_loaded = [sem(f"v_loaded{i}", at) for i in range(2)]
            x_ready = sem("x_ready", at)
            max_done = sem("max_done", at)
            negmax_done = sem("negmax_done", at)
            max_turned = sem("max_turned", at)
            max_copied = sem("max_copied", at)
            max_set = sem("max_set", at)
            scores_ready = sem("scores_ready", at)
            exp_done = sem("exp_done", at)
            pair_done = sem("pair_done", at)
            pv_done = sem("pv_done", at)
            den_done = sem("den_done", at)
            o_copied = sem("o_copied", at)
            den_copied = sem("den_copied", at)
            den_moved = sem("den_moved", at)
            inv_done = sem("inv_done", at)
            inv_moved = sem("inv_moved", at)
            inv_spread = sem("inv_spread", at)
            tm_loaded = sem("tm_loaded", at)
            res_loaded = [sem(f"res_loaded{i}", at) for i in range(2)]
            norm_done = sem("norm_done", at)
            rs2_done = sem("rs2_done", at)
            y8_turned = sem("y8_turned", at)
            y8_copied = sem("y8_copied", at)
            ffn_done = sem("ffn_done", at)
            ffn_added = sem("ffn_added", at)
            out_stored = sem("out_stored", at)
            STACK_DMAS = 4 + 4 * TH
            NORM_STEPS = 14

            def real(n):
                return not isinstance(n, int) or 0 <= n < NQ

            def loads_of_parity(m, p):
                return 8 * (m - p) + 16

            def maxima_at(n, k):
                return (n + 1, 1, k - XLEAD) if k >= XLEAD else (n, 0, k + NSLOT - XLEAD)

            X_BANK_OF = [i % XB for i in range(NSLOT - 1)] + [1]

            def x_bank_freed(i):
                return max(t for t in range(-XB - 2, i) if X_BANK_OF[t] == X_BANK_OF[i])

            def tile_of_max(i):
                return i // 32, i % 32 // 8, i % 8 // 2, i % 2

            def run(eng, period):
                for n in range(-2, 2):
                    period(n, n % 2)
                with eng.Fori(1, NQ // 2 - 1) as i:
                    period(2 * i, 0)
                    period(2 * i + 1, 1)
                for n in range(NQ - 2, NQ + 2):
                    period(n, n % 2)

            with nc.Block() as block:
                @block.tensor
                def _(pe):
                    def scores(n, p, k):
                        th, j, h = k // 32, k % 32 // QH, k % QH
                        if j == 0 and h == 0:
                            pe.wait_ge(max_set, 16 * (2 * n + th + 1))
                        if counted(NSLOT * n + k - 1):
                            pe.wait_ge(exp_done, NSLOT * n + k - 1)
                        nc.tensor.matmul(s_bank[k % 2][:, :], k_st[p][0:KS, h, j * P:(j + 1) * P],
                                         q_st[p][0:KS, th, h, :], start=True, stop=True).then_inc(scores_ready, 1)

                    def scores_for_max(m, p, i):
                        th, h, tc, sh = tile_of_max(i)
                        if i == 0:
                            pe.wait_ge(stacked, 16 * STACK_DMAS * (m + 1))
                        if counted(2 * NSLOT * m + 2 * (x_bank_freed(i) + 1)):
                            pe.wait_ge(max_done, 2 * NSLOT * m + 2 * (x_bank_freed(i) + 1))
                        nc.tensor.matmul(x_bank[X_BANK_OF[i]][:, :], q_st[p][0:KX, th, h, tc * P:(tc + 1) * P],
                                         k_st[p][0:KX, h, sh * HALF:(sh + 1) * HALF],
                                         start=True, stop=True).then_inc(x_ready, 1)

                    def times_v(m, p, c):
                        th, j = c // SJ, c % SJ
                        if c == 0:
                            pe.wait_ge(v_loaded[p], loads_of_parity(m, p))
                        if j == 0:
                            if counted(2 * m + th):
                                pe.wait_ge(o_copied, 2 * m + th)
                        pe.wait_ge(exp_done, NSLOT * m + QH * (c + 1))
                        for h in range(QH):
                            last = nc.tensor.matmul(o_bank[D * h:D * (h + 1), :], v_t[p][:, j, D * h:D * (h + 1)],
                                                    probs[:, c % PR, h, :], start=(j == 0), stop=(j == SJ - 1))
                        last.then_inc(pv_done, 1)

                    def denominators(m, r):
                        th, i = r // 4, r % 4
                        if i == 0:
                            if counted(2 * m + th):
                                pe.wait_ge(den_copied, 2 * m + th)
                        pe.wait_ge(pair_done, SJ * m + r + 1)
                        for h in range(QH):
                            last = nc.tensor.matmul(d_bank[D * h:D * (h + 1), :], ones[:, :], pair_sum[:, r % 2, h, :],
                                                    start=(i == 0), stop=(i == 3))
                        last.then_inc(den_done, 1)

                    def turn_max(m, th):
                        pe.wait_ge(negmax_done, 3 * (2 * m + th + 1))
                        if counted(2 * m + th):
                            pe.wait_ge(max_copied, 2 * m + th)
                        if counted(2 * (m - 3) + 2 if th == 0 else 2 * (m - 2) + 1):
                            pe.wait_ge(ffn_added, 2 * (m - 3) + 2 if th == 0 else 2 * (m - 2) + 1)
                        nc.tensor.matmul(f_bank[:, 0:P], neg_max[:, :], ident_r[:, :], start=True,
                                         stop=True).then_inc(max_turned, 1)

                    def turn_y8(m):
                        pe.wait_ge(norm_done, NORM_STEPS * (m + 1))
                        if real(m + 2):
                            pe.wait_ge(max_copied, 2 * (m + 2) + 1)
                        else:
                            pe.wait_ge(ffn_added, 2 * m)
                        for kc in range(KC):
                            last = nc.tensor.transpose(f_bank_b[:, kc * P:(kc + 1) * P], y8[:, kc * P:(kc + 1) * P],
                                                       ident_b[:, :])
                        last.then_inc(y8_turned, 1)

                    def ffn(m, half, kc):
                        if kc == 0:
                            pe.wait_ge(y8_copied, m + 1)
                            if half == 1 and real(m + 2):
                                pe.wait_ge(max_copied, 2 * (m + 2) + 2)
                            elif half == 1:
                                pe.wait_ge(ffn_added, 2 * m + 1)
                        last = nc.tensor.matmul(f_bank[:, :], y8_t[:, kc, :], w2q[:, kc, half * HALF:(half + 1) * HALF],
                                                start=(kc == 0), stop=(kc == KC - 1))
                        if kc == KC - 1:
                            last.then_inc(ffn_done, 1)

                    def period(n, p):
                        for k in range(NSLOT):
                            m, odd, i = maxima_at(n, k)
                            scores_first = k % 8 not in (0, 5)
                            if real(n) and scores_first:
                                scores(n, p, k)
                            if real(m):
                                scores_for_max(m, (p + odd) % 2, i)
                            if real(n) and not scores_first:
                                scores(n, p, k)
                            if k % 8 == 0:
                                if k >= 8 and real(n):
                                    times_v(n, p, (k - 8) // 4)
                                if k < 8 and real(n - 1):
                                    times_v(n - 1, 1 - p, 14)
                            if k % 8 == 5:
                                if k >= 13 and real(n):
                                    times_v(n, p, (k - 9) // 4)
                                if k < 13 and real(n - 1):
                                    times_v(n - 1, 1 - p, 15)
                            if k % 8 == 2:
                                if k >= 18 and real(n):
                                    denominators(n, (k - 18) // 8)
                                if k < 18 and real(n - 1):
                                    denominators(n - 1, 6 + k // 8)
                            if k == 24 and real(n):
                                turn_max(n, 1)
                            if k == 54 and real(n + 1):
                                turn_max(n + 1, 0)
                            if k == 10 and real(n - 2):
                                turn_y8(n - 2)
                            if 13 <= k < 13 + KC and real(n - 2):
                                ffn(n - 2, 0, k - 13)
                            if 27 <= k < 27 + KC and real(n - 2):
                                ffn(n - 2, 1, k - 27)

                    run(pe, period)

                @block.scalar
                def _(act):
                    def exp(n, k):
                        c, h = k // QH, k % QH
                        if h == 0:
                            if counted(2 * SJ * n + c - PR + 1):
                                act.wait_ge(pv_done, 2 * SJ * n + c - PR + 1)
                            if counted(SJ * n + c // 2 - PR // 2 + 1):
                                act.wait_ge(pair_done, SJ * n + c // 2 - PR // 2 + 1)
                        act.wait_ge(scores_ready, NSLOT * n + k + 1)
                        nc.scalar.activation(probs[:, c % PR, h, :], s_bank[k % 2][:, :], ACT.Exp).then_inc(exp_done, 1)

                    def copy_o(m, th):
                        act.wait_ge(pv_done, 2 * SJ * m + SJ * (th + 1))
                        if counted(NORM_STEPS * (m - 1) + 1):
                            act.wait_ge(norm_done, NORM_STEPS * (m - 1) + 1)
                        nc.scalar.activation(o_raw[:, th], o_bank[:, :], ACT.Copy).then_inc(o_copied, 1)

                    def copy_den(m, th):
                        act.wait_ge(den_done, SJ * m + 4 * (th + 1))
                        if counted(16 * (2 * m + th)):
                            act.wait_ge(den_moved, 16 * (2 * m + th))
                        nc.scalar.activation(den[:, :], d_bank[:, :], ACT.Copy).then_inc(den_copied, 1)

                    def copy_max(m, th):
                        act.wait_ge(max_turned, 2 * m + th + 1)
                        if counted(16 * (2 * m + th)):
                            act.wait_ge(max_set, 16 * (2 * m + th))
                        nc.scalar.activation(max_rows[:, :], f_bank[0:2 * QH * TC, 0:P], ACT.Copy).then_inc(max_copied, 1)

                    def copy_y8(m):
                        act.wait_ge(y8_turned, m + 1)
                        act.wait_ge(ffn_done, 2 * m)
                        nc.scalar.activation(y8_t[:, :, :].rearrange("p k m -> p (k m)"), f_bank_b, ACT.Copy).then_inc(y8_copied, 1)

                    def period(n, p):
                        for k in range(NSLOT):
                            if real(n):
                                exp(n, k)
                            if k == 6 and real(n - 1):
                                copy_o(n - 1, 1)
                            if k == 11 and real(n - 2):
                                copy_y8(n - 2)
                            if k == 13 and real(n - 1):
                                copy_den(n - 1, 1)
                            if k == 25 and real(n):
                                copy_max(n, 1)
                            if k == 38 and real(n):
                                copy_o(n, 0)
                            if k == 44 and real(n):
                                copy_den(n, 0)
                            if k == 55 and real(n + 1):
                                copy_max(n + 1, 0)

                    run(act, period)

                @block.vector
                def _(dve):
                    def maximum(m, i):
                        th, h, tc, sh = tile_of_max(i)
                        if i % 32 == 0:
                            if counted(3 * (2 * m + th - 1)):
                                dve.wait_ge(negmax_done, 3 * (2 * m + th - 1))
                        dve.wait_ge(x_ready, NSLOT * m + i + 1)
                        at = h * TC + tc
                        nc.vector.tensor_reduce(part_max[:, th, sh, at:at + 1], x_bank[X_BANK_OF[i]][:, :], AX,
                                                ALU.max).then_inc(max_done, 2)

                    def negate_max(m, th):
                        done = 3 * (2 * m + th)
                        dve.wait_ge(max_done, 2 * (NSLOT * m + 32 * (th + 1)))
                        dve.wait_ge(init_done, 1)
                        if counted(done):
                            dve.wait_ge(negmax_done, done)
                        nc.vector.tensor_tensor(row_max[:, :], part_max[:, th, 0], part_max[:, th, 1], ALU.max).then_inc(negmax_done, 1)
                        dve.wait_ge(negmax_done, done + 1)
                        if counted(2 * m + th):
                            dve.wait_ge(max_turned, 2 * m + th)
                        R = QH * TC
                        nc.vector.tensor_scalar(neg_max[:, 0:R], row_max[:, :], -1.0, None, ALU.mult).then_inc(negmax_done, 1)
                        dve.wait_ge(negmax_done, done + 2)
                        nc.vector.scalar_tensor_tensor(neg_max[:, R:2 * R], row_max[:, :], -1.0, neg_max[:, 0:R].bitcast(F32),
                                                       ALU.mult, ALU.subtract).then_inc(negmax_done, 1)

                    def invert(m, th):
                        done = 2 * (2 * m + th)
                        dve.wait_ge(den_moved, 16 * (2 * m + th + 1))
                        if counted(16 * (2 * m + th)):
                            dve.wait_ge(inv_moved, 16 * (2 * m + th))
                        nc.vector.reciprocal(inv_c[:, :], den_c[:, :]).then_inc(inv_done, 1)
                        dve.wait_ge(inv_done, done + 1)
                        dve.wait_ge(tm_loaded, 16 * TH * (m + 1))
                        nc.vector.scalar_tensor_tensor(inv_c[:, :], inv_c[:, :], g1[:, 0:1], tm_c[:, th], ALU.mult,
                                                       ALU.mult).then_inc(inv_done, 1)

                    def norm(m, p, step):
                        x1 = res[p]
                        if step != 4:
                            dve.wait_ge(norm_done, NORM_STEPS * m + step)
                        if step in (2, 3):
                            ins = nc.vector.bn_stats(st2[:, step - 2], x1[:, (step - 2) * HALF:(step - 1) * HALF])
                        elif step == 4:
                            ins = nc.vector.bn_aggr(mv2[:, :], st2[:, :, :])
                        elif step == 5:
                            if counted(m):
                                dve.wait_ge(rs2_done, m)
                            ins = nc.vector.tensor_scalar(ve2[:, :], mv2[:, 1:2], EPS, None, ALU.add)
                        elif step == 6:
                            dve.wait_ge(rs2_done, m + 1)
                            ins = nc.vector.tensor_tensor(rss[:, :], rs2[:, :], scl[:, :], ALU.mult)
                        elif step == 7:
                            ins = nc.vector.tensor_scalar(y[:, :], x1[:, :], mv2[:, 0:1], rss[:, 0:1], ALU.subtract, ALU.mult)
                        else:
                            if step == 11:
                                dve.wait_ge(y8_turned, m)
                            ins = f8_step(step - 8, y[:, :], big[:, :], y8[:, :], isnan[:, :])
                        ins.then_inc(norm_done, 1)

                    def add_ffn(m, p, half):
                        s = slice(half * HALF, (half + 1) * HALF)
                        dve.wait_ge(ffn_done, 2 * m + half + 1)
                        nc.vector.scalar_tensor_tensor(res[p][:, s], f_bank[:, :], g2[:, 0:1], res[p][:, s], ALU.mult,
                                                       ALU.add).then_inc(ffn_added, 1)

                    NORM_AT = {35: 2, 37: 3, 38: 4, 39: 5, 43: 6, 45: 7, 48: 8, 53: 9, 58: 10}
                    NORM_AT_2 = {2: 11, 5: 12, 7: 13}

                    def period(n, p):
                        for k in range(NSLOT):
                            m, odd, i = maxima_at(n, k)
                            if NORM_AT.get(k) == 4 and real(n - 1):
                                dve.wait_ge(norm_done, NORM_STEPS * (n - 1) + 4)
                            if real(m):
                                maximum(m, i)
                            if k == 21 and real(n - 2):
                                add_ffn(n - 2, p, 0)
                            if k == 16 and real(n - 1):
                                invert(n - 1, 1)
                            if k == 40 and real(n - 2):
                                add_ffn(n - 2, p, 1)
                            if k == 18 and real(n):
                                negate_max(n, 1)
                            if k == 48 and real(n):
                                invert(n, 0)
                            if k == 50 and real(n + 1):
                                negate_max(n + 1, 0)
                            if k in NORM_AT and real(n - 1):
                                norm(n - 1, 1 - p, NORM_AT[k])
                            if k in NORM_AT_2 and real(n - 2):
                                norm(n - 2, p, NORM_AT_2[k])

                    run(dve, period)

                @block.gpsimd
                def _(pool):
                    def add_pair(n, r):
                        pool.wait_ge(exp_done, NSLOT * n + 2 * QH * (r + 1))
                        if counted(SJ * n + r - 1):
                            pool.wait_ge(den_done, SJ * n + r - 1)
                        a = 2 * r % PR
                        nc.gpsimd.tensor_tensor(pair_sum[:, r % 2], probs[:, a], probs[:, a + 1], ALU.add).then_inc(pair_done, 1)

                    def weigh(m):
                        if counted(NORM_STEPS * m):
                            pool.wait_ge(norm_done, NORM_STEPS * m)
                        pool.wait_ge(o_copied, 2 * (m + 1))
                        pool.wait_ge(inv_spread, 16 * 2 * (m + 1))
                        nc.gpsimd.tensor_tensor(y[:, :], o_raw[:, :, :].rearrange("p a t -> p (a t)"),
                                                inv_b[:, :, :].rearrange("p a t -> p (a t)"), ALU.mult).then_inc(norm_done, 1)

                    def add_residual(m, p):
                        pool.wait_ge(norm_done, NORM_STEPS * m + 1)
                        pool.wait_ge(res_loaded[p], loads_of_parity(m, p))
                        nc.gpsimd.tensor_tensor(res[p][:, :], res[p][:, :], y[:, :], ALU.add).then_inc(norm_done, 1)

                    def period(n, p):
                        for r in range(SJ):
                            if r == 2 and real(n - 1):
                                weigh(n - 1)
                            if real(n):
                                add_pair(n, r)
                            if r == 2 and real(n - 1):
                                add_residual(n - 1, 1 - p)
                            if r == 3 and real(n - 1):
                                pool.wait_ge(norm_done, NORM_STEPS * (n - 1) + 6)
                                nc.gpsimd.tensor_tensor(rs2[:, :], ve2[:, :], neg_half[:, 0:1], ALU.pow).then_inc(rs2_done, 1)

                    nc.gpsimd.memset(neg_max[:, :].bitcast(F32), 0.0).then_inc(init_done, 1)
                    run(pool, period)

                @block.sync
                def _(sp):
                    qx_q = qx_scr.rearrange("r b q t -> r (b q) t")
                    kx_q = kx_scr.rearrange("r b q t -> r (b q) t")
                    tm_q = tm_scr.rearrange("b q t -> (b q) t")

                    def stack(m, p):
                        if counted(NSLOT * (m - 1)):
                            sp.wait_ge(scores_ready, NSLOT * (m - 1))
                        if counted(NSLOT * (m - 1)):
                            sp.wait_ge(x_ready, NSLOT * (m - 1))
                        rows = bass.ds(m * P, P)
                        k_part = [k_scr[part, rows, :].rearrange("(h d) s -> d h s", d=D) for part in range(2)]
                        q_part = [q_scr[part, rows, :].rearrange("(h d) (a t) -> d a h t", d=D, a=TH) for part in range(2)]
                        for at, part in ((0, 0), (D, 1), (2 * D, 0)):
                            sp.dma_start(k_st[p][at:at + D, :, :].bitcast(F32), k_part[part]).then_inc(stacked, 16)
                        sp.dma_start(k_st[p][96:KS, :, :].bitcast(F32), kx_q[:, bass.ds(m, 1), :].broadcast_to((4, QH, S))).then_inc(stacked, 16)
                        for at, part in ((0, 0), (D, 0), (2 * D, 1)):
                            for th in range(TH):
                                sp.dma_start(q_st[p][at:at + D, th, :, :].bitcast(F32), q_part[part][:, th]).then_inc(stacked, 16)
                        for th in range(TH):
                            row = qx_q[:, bass.ds(m, 1), th * HALF:(th + 1) * HALF]
                            sp.dma_start(q_st[p][96:98, th, :, :].bitcast(F32), row.broadcast_to((2, QH, HALF))).then_inc(stacked, 16)

                    def load_v(m, p):
                        if counted(2 * SJ * (m - 1)):
                            sp.wait_ge(pv_done, 2 * SJ * (m - 1))
                        sp.dma_start(v_t[p][:, :, :], v_scr[bass.ds(m, 1), :, :].rearrange("o (j s) d -> s (o j) d", s=P)).then_inc(v_loaded[p], 16)

                    def move_den(m, th):
                        sp.wait_ge(den_copied, 2 * m + th + 1)
                        sp.dma_start(den_c[:, :], den[0:P:D, :]).then_inc(den_moved, 16)

                    def move_inv(m, th):
                        sp.wait_ge(inv_done, 2 * (2 * m + th + 1))
                        sp.dma_start(inv_scr[th].rearrange("h (u v) -> (h u) v", u=D), inv_c[:, :]).then_inc(inv_moved, 16)
                        sp.wait_ge(inv_moved, 16 * (2 * m + th + 1))
                        if counted(NORM_STEPS * (m - 1) + 1):
                            sp.wait_ge(norm_done, NORM_STEPS * (m - 1) + 1)
                        sp.dma_start(inv_b[:, th, :], inv_scr[th].unsqueeze(1).broadcast_to((QH, D, HALF))).then_inc(inv_spread, 16)

                    def load_tm(m):
                        if counted(16 * 2 * m):
                            sp.wait_ge(inv_spread, 16 * 2 * m)
                        for th in range(TH):
                            row = tm_q[bass.ds(m, 1), th * HALF:(th + 1) * HALF]
                            sp.dma_start(tm_c[:, th, :], row.broadcast_to((QH, HALF))).then_inc(tm_loaded, 16)

                    def set_max(m, th, p):
                        sp.wait_ge(max_copied, 2 * m + th + 1)
                        sp.dma_start(q_st[p][KX:KS, th, :, :].bitcast(F32), max_rows[:, :].bitcast(F32)).then_inc(max_set, 16)

                    def load_res(m, p):
                        if counted(16 * (m - 1)):
                            sp.wait_ge(out_stored, 16 * (m - 1))
                        sp.dma_start(res[p][:, :], x_rows[bass.ds(m * P, P), :]).then_inc(res_loaded[p], 16)

                    def store(m, p):
                        sp.wait_ge(ffn_added, 2 * (m + 1))
                        sp.dma_start(out_rows[bass.ds(m * P, P), :], res[p][:, :]).then_inc(out_stored, 16)

                    def period(n, p):
                        if real(n + 1):
                            stack(n + 1, 1 - p)
                            load_v(n + 1, 1 - p)
                        if real(n - 1):
                            move_den(n - 1, 1)
                            move_inv(n - 1, 1)
                        if real(n):
                            load_tm(n)
                        if real(n):
                            set_max(n, 1, p)
                        if real(n - 2):
                            store(n - 2, p)
                        if real(n):
                            move_den(n, 0)
                            move_inv(n, 0)
                        if real(n + 1):
                            set_max(n + 1, 0, 1 - p)
                        if real(n):
                            load_res(n, p)

                    run(sp, period)
                    sp.wait_ge(out_stored, 16 * NQ)


_INS = ['x', 'ctx_2048', 'mask_Bx1x2048_fk1', 'g_xattn', 'g_ffn', 'L0_xattn_Wq', 'L0_xattn_bq', 'L0_xattn_Wk',
        'L0_xattn_bk', 'L0_xattn_Wv', 'L0_xattn_bv', 'L0_ffn_input2', 'L0_ffn_scale', 'L0_ffn_scale1']


def kernel(**inputs):
    import numpy as _np
    import concourse.bacc as _bacc
    from concourse import mybir as _mybir
    from concourse.bass_utils import run_bass_kernel_spmd as _run

    nc = _bacc.Bacc("TRN2", target_bir_lowering=False, num_devices=1)
    arrays, args = {}, []
    for name in _INS:
        a = _np.ascontiguousarray(inputs[name])
        arrays[f"in_{name}_dram"] = a
        args.append(nc.dram_tensor(f"in_{name}_dram", a.shape, _mybir.dt.from_np(a.dtype), kind="ExternalInput").ap())
    shape = arrays["in_x_dram"].shape
    args.append(nc.dram_tensor("out_0_dram", shape, _mybir.dt.float32, kind="ExternalOutput").ap())
    flamingo_gated_layer(nc, *args)
    r = _run(nc, [arrays], core_ids=[0])
    return r.results[0]["out_0_dram"]
```
